# Optimizing a Trainium2 kernel written in Bass

```python
import numpy as np
import jax
import jax.numpy as jnp

def _softmax(x, axis=-1):
    return jax.nn.softmax(x, axis=axis)

def _gelu(x):
    return jax.nn.gelu(x, approximate=True)

def _silu(x):
    return jax.nn.silu(x)

def _sigmoid(x):
    return jax.nn.sigmoid(x)

def _layernorm(x, axis=-1, eps=1e-05):
    m = jnp.mean(x, axis=axis, keepdims=True)
    v = jnp.var(x, axis=axis, keepdims=True)
    return (x - m) / jnp.sqrt(v + eps)

def _scatter_add(tgt, idx, src, axis=0):
    return tgt.at[idx].add(src)

def _segment_sum(src, seg, n):
    return jax.ops.segment_sum(src, seg, n)
kernel_name = 'mk_cond_resid_d2_seqx_r4_a6ac93'

def setup_inputs(seed: int=0):
    np.random.seed(seed)
    _w = jnp.asarray

    def _rec_inputs():
        import jax
        import jax.numpy as jnp
        _rk = jax.random.key(seed)
        x = -0.000125 + 0.9999 * jax.random.normal(jax.random.fold_in(_rk, 1), (2, 1024, 256), jnp.float32)
        _lenS = 1024 - jax.random.randint(jax.random.fold_in(_rk, 7), (2,), 0, max(1, 1024 // 4) + 1, jnp.int32)
        _lenS2 = 1024 - jax.random.randint(jax.random.fold_in(_rk, 8), (2,), 0, max(1, 1024 // 4) + 1, jnp.int32)
        cond_1024 = 0.00513981 + 1.0024 * jax.random.normal(jax.random.fold_in(_rk, 11), (2, 256), jnp.float32)
        return (x, cond_1024)
    x, cond_1024 = _rec_inputs()

    def _L0_cond_setup():
        import jax, jax.numpy as jnp
        import numpy as np
        IN_FEATURES = 256
        OUT_FEATURES = 256
        BATCH = 32
        SEQ = 256
        EPS = 1e-08
        key = jax.random.key(seed)
        k1, k2, k3 = jax.random.split(key, 3)
        Efou = jax.random.normal(k1, (BATCH, SEQ, IN_FEATURES), dtype=jnp.float32)
        y = jax.random.normal(k2, (BATCH, IN_FEATURES), dtype=jnp.float32)
        weight = jax.random.normal(k3, (IN_FEATURES, OUT_FEATURES), dtype=jnp.float32)
        return {'Efou': Efou, 'y': y, 'weight': weight}
    _L0_cond_all = _L0_cond_setup()
    _L0_cond_in = {k: v for k, v in _L0_cond_all.items() if k in ('weight',)}
    del _L0_cond_all

    def _L1_cond_setup():
        import jax, jax.numpy as jnp
        import numpy as np
        import math
        N, T, D, H = (64, 128, 256, 256)
        key = jax.random.key(seed)
        k1, k2, k3, k4 = jax.random.split(key, 4)
        x = jax.random.normal(k1, (N, T, D), dtype=jnp.float32)
        h0 = jax.random.normal(k2, (N, H), dtype=jnp.float32)
        Wx = jax.random.normal(k3, (D, 4 * H), dtype=jnp.float32) / math.sqrt(D)
        Wh = jax.random.normal(k4, (H, 4 * H), dtype=jnp.float32) / math.sqrt(H)
        b = jnp.zeros((4 * H,), dtype=jnp.float32)
        return {'x': x, 'h0': h0, 'Wx': Wx, 'Wh': Wh, 'b': b}
    _L1_cond_all = _L1_cond_setup()
    _L1_cond_in = {k: v for k, v in _L1_cond_all.items() if k in ('Wx', 'Wh', 'b')}
    del _L1_cond_all
    return {'x': x, 'cond_1024': cond_1024, 'L0_cond_weight': _L0_cond_in['weight'], 'L1_cond_Wx': _L1_cond_in['Wx'], 'L1_cond_Wh': _L1_cond_in['Wh'], 'L1_cond_b': _L1_cond_in['b']}

def reference(x, cond_1024, L0_cond_weight, L1_cond_Wx, L1_cond_Wh, L1_cond_b):
    import jax
    import jax.numpy as jnp

    def _L0_cond_ref(Efou, y, weight):
        import jax, jax.numpy as jnp
        import numpy as np
        IN_FEATURES = 256
        OUT_FEATURES = 256
        BATCH = 32
        SEQ = 256
        EPS = 1e-08
        scale = 1.0 / np.sqrt(np.float32(weight.shape[0]))
        ys = y * scale
        d = jax.lax.rsqrt(jnp.einsum('bi,io->bo', ys * ys, weight * weight) + EPS)
        out = jnp.einsum('bsi,io->bso', Efou * ys[:, None, :], weight) * d[:, None, :]
        return out

    def _L1_cond_ref(x, h0, Wx, Wh, b):
        import jax, jax.numpy as jnp
        import numpy as np
        import math
        N, T, D, H = (64, 128, 256, 256)
        Hdim = h0.shape[1]
        c0 = jnp.zeros_like(h0)
        xW = jnp.einsum('ntd,dk->tnk', x, Wx) + b

        def step(carry, xw_t):
            prev_h, prev_c = carry
            a = xw_t + prev_h @ Wh
            i = jax.nn.sigmoid(a[:, :Hdim])
            f = jax.nn.sigmoid(a[:, Hdim:2 * Hdim])
            o = jax.nn.sigmoid(a[:, 2 * Hdim:3 * Hdim])
            g = jnp.tanh(a[:, 3 * Hdim:])
            next_c = f * prev_c + i * g
            next_h = o * jnp.tanh(next_c)
            return ((next_h, next_c), next_h)
        _, hs = jax.lax.scan(step, (h0, c0), xW)
        return jnp.transpose(hs, (1, 0, 2))
    x = x + _L0_cond_ref(x, cond_1024, L0_cond_weight)
    x = x + _L1_cond_ref(x, cond_1024, L1_cond_Wx, L1_cond_Wh, L1_cond_b)
    return x

_drawn_inputs = setup_inputs


def setup_inputs(seed=0):
    import zlib

    import numpy as np

    out = dict(_drawn_inputs(seed))
    spreads = {'L1_cond_b': (0.0, 0.355)}
    factors = {}
    for name, (base, spread) in spreads.items():
        noise = np.random.default_rng([zlib.crc32(name.encode()), seed]).standard_normal(out[name].shape)
        drawn = base * np.exp(spread * noise) if base else spread * noise
        out[name] = jnp.asarray(drawn.astype(out[name].dtype))
    for name, factor in factors.items():
        out[name] = (out[name] * factor).astype(out[name].dtype)
    return out
```

```python
from contextlib import ExitStack

import concourse.bass as bass
from concourse import mybir

F32 = mybir.dt.float32
F16 = mybir.dt.float16
BF16 = mybir.dt.bfloat16
U32 = mybir.dt.uint32
ALU = mybir.AluOpType
ACT = mybir.ActivationFunctionType
AX = mybir.AxisListType

P = 128
BANK = 512
UNROLL = 8
HALF = UNROLL // 2
EPS = 1e-8
H_SCALE = 12
W_TOP = 14
EXPONENT = 0x7F800000
GATE_I, GATE_F, GATE_O, GATE_G = range(4)


def cond_resid_lstm(nc, x, cond, w, wx, wh, bias, out):
    B, T, D = x.shape
    K = D // P
    M = wx.shape[1] // P
    G = M // K
    CB = K * B
    NT = T // P
    NB = T // BANK
    NSMALL = B * K + M
    assert D == K * P and G == 4 and T % BANK == 0 and T % UNROLL == 0

    with ExitStack() as ctx:
        def sb(name, shape, dt=F32):
            return ctx.enter_context(nc.sbuf_tensor(name, shape, dt))

        def sem(name):
            return ctx.enter_context(nc.semaphore(name))

        x_rows = sb("x_rows", [P, B * NT, D])
        w_sb = sb("w_sb", [P, K, D])
        wx_sb = sb("wx_sb", [P, K, G * D])
        wh_sb = sb("wh_sb", [P, K, G * D])
        small_rows = sb("small_rows", [NSMALL, P])
        ident = sb("ident", [P, P])
        ident_b = sb("ident_b", [P, P], BF16)
        ones_row = sb("ones_row", [1, P])
        small = sb("small", [P, NSMALL])
        ys = sb("ys", [P, B, K])
        ys2 = sb("ys2", [P, B, K])
        w2 = sb("w2", [P, K, D])
        wy = sb("wy", [P, B, K, D])
        var = sb("var", [P, CB])
        root = sb("root", [P, CB])
        d0 = sb("d0", [P, CB])
        d_tmp = sb("d_tmp", [P, 3, CB])
        d_sb = sb("d_sb", [P, CB])
        wmax = sb("wmax", [P, 1])
        wmax1 = sb("wmax1", [1, 2])
        scales_row = sb("scales_row", [1, 2])
        scales = sb("scales", [P, 2])
        w_scale = sb("w_scale", [P, 1])
        bias_s = sb("bias_s", [P, M])
        h0wh = sb("h0wh", [P, M, B])
        xt = sb("xt", [P, K, B, T])
        xw = sb("xw", [P, M, B, T])
        wh_s = sb("wh_s", [P, K, G * D])
        wh_p = sb("wh_p", [P, 2, K, G * D], F16)

        ring = sb("ring", [P, UNROLL, G, 3, CB], BF16)
        rest = sb("rest", [P, M * B, HALF])
        hring = sb("hring", [P, UNROLL, CB])
        hsave = sb("hsave", [P, 2, CB, HALF])
        hp = sb("hp", [P, K, 2, B], F16)
        pre_f = sb("pre_f", [P, CB])
        pre_g = sb("pre_g", [P, CB])
        sig_f = sb("sig_f", [P, CB])
        sig_o = sb("sig_o", [P, CB])
        scan_a = sb("scan_a", [P, CB, 2])
        scan_b = sb("scan_b", [P, CB, 2])
        cell = sb("cell", [P, CB, 2])
        tanh_c = sb("tanh_c", [P, CB])
        y_rows = sb("y_rows", [P, B * NT, D])

        banks = [ctx.enter_context(nc.psum_tensor(f"bank{i}", [P, BANK], F32)) for i in range(8)]

        s_x = [sem(f"s_x{b}") for b in range(B)]
        s_w, s_wx, s_wh, s_small = sem("s_w"), sem("s_wx"), sem("s_wh"), sem("s_small")
        s_zero, s_ident, s_identb, s_ones = sem("s_zero"), sem("s_ident"), sem("s_identb"), sem("s_ones")
        s_filled = sem("s_filled")
        s_act, s_dve = sem("s_act"), sem("s_dve")
        s_ys, s_ys2, s_w2, s_wy = sem("s_ys"), sem("s_ys2"), sem("s_w2"), sem("s_wy")
        s_wmax, s_scales = sem("s_wmax"), sem("s_scales")
        s_chain = sem("s_chain")
        s_bias, s_var, s_whs, s_hi = sem("s_bias"), sem("s_var"), sem("s_whs"), sem("s_hi")
        s_setup = sem("s_setup")
        s_pool = sem("s_pool")
        ring_full, ring_used = sem("ring_full"), sem("ring_used")
        hring_saved, h_seen = sem("hring_saved"), sem("h_seen")
        h_hi, h_lo, h_all = sem("h_hi"), sem("h_lo"), sem("h_all")
        f_mm, g_mm, i_mm, o_mm = sem("f_mm"), sem("g_mm"), sem("i_mm"), sem("o_mm")
        f_sum, g_sum = sem("f_sum"), sem("g_sum")
        f_act, g_act, i_act, o_act = sem("f_act"), sem("g_act"), sem("i_act"), sem("o_act")
        fc_done, c_done, t_done = sem("fc_done"), sem("c_done"), sem("t_done")
        y_filled, y_act, y_dve, s_out = sem("y_filled"), sem("y_act"), sem("y_dve"), sem("s_out")

        groups = [(("small",), "act"), (("wmax",), "dve")]
        groups += [(("xt", b, k, n), "act" if k else "dve") for b in range(B) for n in range(NB) for k in range(K)]
        groups += [(("var",), "dve"), (("scales",), "dve"), (("h0wh",), "dve")]
        groups += [(("x1", b, m, n), "dve") for b in range(B) for n in range(NB) for m in range(K)]
        groups += [(("xw", b, m, n), "act" if m % 2 else "dve") for n in range(NB) for b in range(B) for m in range(M)]
        order = {what: g for g, (what, _) in enumerate(groups)}

        def bank_of(what):
            return banks[order[what] % 8]

        def read_out(g):
            who = groups[g][1]
            return (s_act if who == "act" else s_dve), sum(1 for _, e in groups[:g + 1] if e == who)

        def last_read(kind):
            found = {}
            for g, (what, who) in enumerate(groups):
                if what[0] == kind:
                    found[who] = read_out(g)
            return list(found.values())

        block = ctx.enter_context(nc.Block())

        @block.sync
        def _(sp):
            sp.dma_start(small_rows[0:B * K, :], cond.rearrange("b (k p) -> (b k) p", p=P)).then_inc(s_small, 16)
            sp.dma_start(small_rows[B * K:NSMALL, :], bias.rearrange("(m p) -> m p", p=P)).then_inc(s_small, 16)
            sp.dma_start(w_sb[:, :, :], w.rearrange("(k p) o -> p k o", p=P)).then_inc(s_w, 16)
            for b in range(B):
                sp.dma_start(x_rows[:, b * NT:(b + 1) * NT, :],
                             x[b].rearrange("(n p) d -> p n d", p=P)).then_inc(s_x[b], 16)
            for j in range(B * NT):
                b, n = divmod(j, NT)
                sp.wait_ge(y_act, j + 1)
                sp.wait_ge(y_dve, j + 1)
                sp.dma_start(out[b, n * P:(n + 1) * P, :], y_rows[:, j, :]).then_inc(s_out, 16)
            sp.wait_ge(s_out, 16 * B * NT)

        @block.gpsimd
        def _(pool):
            nc.gpsimd.memset(ident[:, :], 0.0).then_inc(s_zero, 1)
            nc.gpsimd.memset(ones_row[:, :], 1.0).then_inc(s_ones, 1)
            pool.wait_ge(s_zero, 1)
            nc.gpsimd.affine_select(out=ident[:, :], in_=ident[:, :], compare_op=ALU.not_equal, fill=1.0,
                                    base=0, pattern=[[-1, P]], channel_multiplier=1).then_inc(s_ident, 1)
            pool.wait_ge(s_ident, 1)
            nc.gpsimd.tensor_copy(ident_b[:, :], ident[:, :]).then_inc(s_identb, 1)

            xw_t = xw[:, :, :, :].rearrange("p m b t -> p (m b) t")
            xt_t = xt[:, :, :, :].rearrange("p k b t -> p (k b) t")

            def parts(half, part):
                return ring[:, half * HALF:(half + 1) * HALF, :, part, :].rearrange("p s g c -> p g c s")

            def by_gate(ap):
                return ap.rearrange("p (g c) s -> p g c s", g=G)

            def settle():
                pool.wait_ge(s_pool, 1)
                pool.sem_inc(s_pool, -1)

            def split(half, t0):
                src = by_gate(xw_t[:, :, bass.ds(t0, HALF)])
                res = by_gate(rest[:, :, :])
                nc.gpsimd.tensor_copy(parts(half, 0), src).then_inc(s_pool, 1)
                settle()
                nc.gpsimd.tensor_tensor(res, src, parts(half, 0), ALU.subtract).then_inc(s_pool, 1)
                settle()
                nc.gpsimd.tensor_copy(parts(half, 1), res).then_inc(s_pool, 1)
                settle()
                nc.gpsimd.tensor_tensor(parts(half, 2), res, parts(half, 1), ALU.subtract).then_inc(ring_full, 1)

            def save(half, t0):
                now = xt_t[:, :, bass.ds(t0, HALF)]
                nc.gpsimd.tensor_scalar(hsave[:, half, :, :], hring[:, half * HALF:(half + 1) * HALF, :].rearrange("p s c -> p c s"),
                                        2.0 ** -H_SCALE, None, ALU.mult).then_inc(s_pool, 1)
                settle()
                nc.gpsimd.tensor_tensor(now, now, hsave[:, half, :, :], ALU.add).then_inc(hring_saved, 1)

            nc.gpsimd.memset(rest[:, 0, 0:1], 0.0).then_inc(hring_saved, 2)
            for s, v in last_read("xw"):
                pool.wait_ge(s, v)
            pool.wait_ge(s_setup, 1)
            split(0, 0)
            split(1, HALF)
            with pool.Fori(0, T // UNROLL - 1) as i:
                t = i * UNROLL
                for half in range(2):
                    pool.wait_ge(ring_used, 1)
                    pool.sem_inc(ring_used, -1)
                    split(half, t + UNROLL + half * HALF)
                    pool.wait_ge(h_all, t + (half + 1) * HALF)
                    pool.sem_inc(h_seen, 1)
                    save(half, t + half * HALF)
            for half in range(2):
                pool.wait_ge(h_all, T - UNROLL + (half + 1) * HALF)
                save(half, T - UNROLL + half * HALF)

        @block.tensor
        def _(pe):
            def start_group(what):
                g = order[what]
                if g >= 8:
                    pe.wait_ge(*read_out(g - 8))
                return banks[g % 8]

            def mm(out_, lhs, rhs, first, last):
                return nc.tensor.matmul(out_, lhs, rhs, start=first, stop=last, skip_group_check=True)

            pe.wait_ge(s_ident, 1)
            pe.wait_ge(s_small, 32)
            nc.tensor.transpose(start_group(("small",))[:, 0:NSMALL], small_rows[:, :],
                                ident[0:NSMALL, 0:NSMALL]).then_inc(s_filled, 1)
            pe.wait_ge(s_wmax, 1)
            nc.tensor.transpose(start_group(("wmax",))[0:1, 0:P], wmax[:, :], ident[:, :]).then_inc(s_filled, 1)
            for b in range(B):
                pe.wait_ge(s_x[b], 16)
                for n in range(NB):
                    for k in range(K):
                        bank = start_group(("xt", b, k, n))
                        for j in range(BANK // P):
                            last = nc.tensor.transpose(bank[:, j * P:(j + 1) * P],
                                                       x_rows[:, b * NT + n * (BANK // P) + j, k * P:(k + 1) * P], ident[:, :])
                        last.then_inc(s_filled, 1)
            bank = start_group(("var",))
            pe.wait_ge(s_ys2, 1)
            pe.wait_ge(s_w2, 1)
            for m in range(K):
                for k in range(K):
                    last = mm(bank[:, m * B:(m + 1) * B], w2[:, k, m * P:(m + 1) * P], ys2[:, :, k], m == 0 and k == 0, k == K - 1)
            last.then_inc(s_filled, 1)
            bank = start_group(("scales",))
            pe.wait_ge(s_scales, 2)
            pe.wait_ge(s_ones, 1)
            mm(bank[:, 0:2], ones_row[:, :], scales_row[:, :], True, True).then_inc(s_filled, 1)
            bank = start_group(("h0wh",))
            pe.wait_ge(s_wh, 16)
            pe.wait_ge(*read_out(order[("small",)]))
            h0 = small[:, 0:B * K].rearrange("p (b k) -> p b k", k=K)
            for m in range(M):
                for k in range(K):
                    last = mm(bank[:, m * B:(m + 1) * B], wh_sb[:, k, m * P:(m + 1) * P], h0[:, :, k], m == 0 and k == 0, k == K - 1)
            last.then_inc(s_filled, 1)
            pe.wait_ge(s_wy, B * K)
            for s, v in last_read("xt"):
                pe.wait_ge(s, v)
            for b in range(B):
                for n in range(NB):
                    for m in range(K):
                        bank = start_group(("x1", b, m, n))
                        for k in range(K):
                            last = mm(bank[:, :], wy[:, b, k, m * P:(m + 1) * P], xt[:, k, b, n * BANK:(n + 1) * BANK], k == 0, k == K - 1)
                        last.then_inc(s_filled, 1)
            pe.wait_ge(s_wx, 16)
            for n in range(NB):
                for b in range(B):
                    for m in range(M):
                        bank = start_group(("xw", b, m, n))
                        if m == 0:
                            pe.wait_ge(*read_out(order[("x1", b, K - 1, n)]))
                        for k in range(K):
                            last = mm(bank[:, :], wx_sb[:, k, m * P:(m + 1) * P], xt[:, k, b, n * BANK:(n + 1) * BANK], k == 0, k == K - 1)
                        last.then_inc(s_filled, 1)

            for s, v in last_read("xw"):
                pe.wait_ge(s, v)
            pe.wait_ge(s_setup, 1)
            pe.wait_ge(s_identb, 1)

            def apart(gate, parity):
                return banks[4 * parity + gate][:, 0:2 * CB].rearrange("p (c q b) -> p c q b", c=K, q=2)

            def together(gate, parity):
                return banks[4 * parity + gate][:, 0:CB].rearrange("p (c b) -> p c b", c=K)

            def products(gate, parity, w_part, h_part, chunks=range(K)):
                for c in chunks:
                    m = gate * K + c
                    for k in range(K):
                        last = mm(together(gate, parity)[:, c, :], wh_p[:, w_part, k, m * P:(m + 1) * P],
                                  hp[:, k, h_part, :], False, True)
                return last

            def products_apart(gate, parity):
                for c in range(K):
                    m = gate * K + c
                    for k in range(K):
                        for w_part in range(2):
                            last = mm(apart(gate, parity)[:, c, :, :], wh_p[:, w_part, k, m * P:(m + 1) * P],
                                      hp[:, k, :, :], False, True)
                return last

            with pe.Fori(0, T // UNROLL) as i:
                t = i * UNROLL
                for u in range(UNROLL):
                    q = u % 2
                    if u % HALF == 0:
                        pe.wait_ge(ring_full, 2 * i + u // HALF + 1)
                    for gate in (GATE_F, GATE_G):
                        last_f = mm(apart(gate, q).rearrange("p c q b -> p q c b"), ident_b[:, :],
                                    ring[:, u, gate, 0:2, :].rearrange("p q (c b) -> p q c b", c=K), True, True)
                        mm(apart(gate, q)[:, :, 0, :], ident_b[:, :],
                           ring[:, u, gate, 2, :].rearrange("p (c b) -> p c b", c=K), False, True)
                    for gate in (GATE_I, GATE_O):
                        for part in range(3):
                            last = mm(together(gate, q), ident_b[:, :],
                                      ring[:, u, gate, part, :].rearrange("p (c b) -> p c b", c=K), part == 0, True)
                    if u % HALF == HALF - 1:
                        last.then_inc(ring_used, 1)
                    pe.wait_ge(h_hi, t + u + 1)
                    products(GATE_I, q, 0, 0)
                    products(GATE_I, q, 1, 0)
                    pe.wait_ge(h_lo, t + u + 1)
                    products_apart(GATE_F, q).then_inc(f_mm, 1)
                    products_apart(GATE_G, q).then_inc(g_mm, 1)
                    products(GATE_I, q, 0, 1)
                    products(GATE_I, q, 1, 1).then_inc(i_mm, 1)
                    products(GATE_O, q, 0, 0)
                    products(GATE_O, q, 1, 0)
                    products(GATE_O, q, 0, 1)
                    products(GATE_O, q, 1, 1).then_inc(o_mm, 1)

            pe.wait_ge(hring_saved, 2 + T // HALF)
            for j in range(B * NT):
                b, n = divmod(j, NT)
                if j >= 4:
                    pe.wait_ge(y_act, j - 3)
                    pe.wait_ge(y_dve, j - 3)
                for k in range(K):
                    last = nc.tensor.transpose(banks[2 * (j % 4) + k][:, 0:P], xt[:, k, b, n * P:(n + 1) * P], ident[:, :])
                last.then_inc(y_filled, 1)

        @block.vector
        def _(dve):
            chain = [0]

            def link(ins):
                chain[0] += 1
                ins.then_inc(s_chain, 1)
                dve.wait_ge(s_chain, chain[0])

            def group(what):
                dve.wait_ge(s_filled, order[what] + 1)
                return bank_of(what)

            dve.wait_ge(s_wh, 16)
            nc.vector.tensor_reduce(wmax[:, :], wh_sb[:, :, :], AX.XY, ALU.max, apply_absolute_value=True).then_inc(s_wmax, 1)
            dve.wait_ge(s_w, 16)
            nc.vector.tensor_tensor(w2[:, :, :], w_sb[:, :, :], w_sb[:, :, :], ALU.mult).then_inc(s_w2, 1)
            dve.wait_ge(*read_out(order[("small",)]))
            link(nc.vector.tensor_scalar(ys[:, :, :], small[:, 0:B * K].rearrange("p (b k) -> p b k", k=K),
                                         1.0 / float(D) ** 0.5, None, ALU.mult))
            nc.vector.tensor_tensor(ys2[:, :, :], ys[:, :, :], ys[:, :, :], ALU.mult).then_inc(s_ys2, 1)
            for b in range(B):
                for k in range(K):
                    nc.vector.tensor_scalar(wy[:, b, k, :], w_sb[:, k, :], ys[:, b, k:k + 1], None, ALU.mult).then_inc(s_wy, 1)
            bank = group(("wmax",))
            nc.vector.tensor_reduce(wmax1[:, 0:1], bank[0:1, 0:P], AX.X, ALU.max).then_inc(s_dve, 1)
            dve.wait_ge(*read_out(order[("wmax",)]))
            link(nc.vector.tensor_scalar(wmax1[:, 0:1], wmax1[:, 0:1], 4.0, None, ALU.max))
            link(nc.vector.tensor_scalar(wmax1[:, 0:1].bitcast(U32), wmax1[:, 0:1].bitcast(U32), EXPONENT, None, ALU.bitwise_and))
            link(nc.vector.tensor_scalar(wmax1[:, 1:2].bitcast(U32), wmax1[:, 0:1].bitcast(U32), EXPONENT, None, ALU.bitwise_xor))
            nc.vector.tensor_scalar(scales_row[:, 0:1], wmax1[:, 1:2], 2.0 ** (W_TOP - 1 + H_SCALE), None, ALU.mult).then_inc(s_scales, 1)
            nc.vector.tensor_scalar(scales_row[:, 1:2], wmax1[:, 0:1], 2.0 ** -(W_TOP + H_SCALE), None, ALU.mult).then_inc(s_scales, 1)
            for b in range(B):
                for n in range(NB):
                    bank = group(("xt", b, 0, n))
                    nc.vector.tensor_copy(xt[:, 0, b, n * BANK:(n + 1) * BANK], bank[:, :]).then_inc(s_dve, 1)
            bank = group(("var",))
            nc.vector.tensor_scalar(var[:, :], bank[:, 0:CB], EPS, None, ALU.add).then_inc(s_dve, 1)
            dve.wait_ge(*read_out(order[("var",)]))
            bank = group(("scales",))
            nc.vector.tensor_copy(scales[:, :], bank[:, 0:2]).then_inc(s_dve, 1)
            dve.wait_ge(*read_out(order[("scales",)]))
            link(nc.vector.tensor_scalar(w_scale[:, :], scales[:, 0:1], 2.0 ** -H_SCALE, None, ALU.mult))
            nc.vector.tensor_scalar(bias_s[:, :], small[:, B * K:NSMALL], scales[:, 0:1], None, ALU.mult).then_inc(s_bias, 1)
            bank = group(("h0wh",))
            nc.vector.tensor_copy(h0wh[:, :, :], bank[:, 0:M * B].rearrange("p (m b) -> p m b", b=B)).then_inc(s_dve, 1)
            dve.wait_ge(s_var, 1)
            link(nc.vector.reciprocal(d0[:, :], root[:, :]))
            link(nc.vector.tensor_tensor(d_tmp[:, 0, :], d0[:, :], d0[:, :], ALU.mult))
            link(nc.vector.tensor_tensor(d_tmp[:, 1, :], d_tmp[:, 0, :], var[:, :], ALU.mult))
            link(nc.vector.tensor_scalar(d_tmp[:, 2, :], d_tmp[:, 1, :], -0.5, 1.5, ALU.mult, ALU.add))
            link(nc.vector.tensor_tensor(d_sb[:, :], d_tmp[:, 2, :], d0[:, :], ALU.mult))
            for b in range(B):
                for n in range(NB):
                    dve.wait_ge(s_filled, order[("x1", b, K - 1, n)] + 1)
                    for s, v in last_read("xt"):
                        dve.wait_ge(s, v)
                    for m in range(K):
                        now = xt[:, m, b, n * BANK:(n + 1) * BANK]
                        nc.vector.scalar_tensor_tensor(out=now, in0=bank_of(("x1", b, m, n))[:, :], scalar=d_sb[:, m * B + b:m * B + b + 1],
                                                       in1=now, op0=ALU.mult, op1=ALU.add).then_inc(s_dve, 1)
            link(nc.vector.tensor_scalar(wh_s[:, :, :], wh_sb[:, :, :], w_scale[:, :], None, ALU.mult))
            link(nc.vector.tensor_copy(wh_p[:, 0, :, :], wh_s[:, :, :]))
            link(nc.vector.tensor_tensor(wh_p[:, 1, :, :], wh_s[:, :, :], wh_p[:, 0, :, :], ALU.subtract))
            dve.wait_ge(s_bias, 1)
            for n in range(NB):
                for b in range(B):
                    for m in range(0, M, 2):
                        bank = group(("xw", b, m, n))
                        nc.vector.tensor_scalar(xw[:, m, b, n * BANK:(n + 1) * BANK], bank[:, :], scales[:, 0:1],
                                                bias_s[:, m:m + 1], ALU.mult, ALU.add).then_inc(s_dve, 1)
            link(nc.vector.memset(scan_a[:, :, :], 0.0))
            link(nc.vector.memset(cell[:, :, :], 0.0))
            nc.vector.memset(hp[:, :, 0, :], 0.0).then_inc(h_hi, 1)
            nc.vector.memset(hp[:, :, 1, :], 0.0).then_inc(h_lo, 1)
            for s, v in last_read("xw"):
                dve.wait_ge(s, v)
            nc.vector.scalar_tensor_tensor(out=xw[:, :, :, 0], in0=h0wh[:, :, :], scalar=scales[:, 0:1],
                                           in1=xw[:, :, :, 0], op0=ALU.mult, op1=ALU.add).then_inc(s_setup, 1)

            def parts_of(gate, parity):
                return banks[4 * parity + gate][:, 0:2 * CB].rearrange("p (c q b) -> p c b q", c=K, q=2)

            def by_chunk(ap):
                return ap.rearrange("p (c b) -> p c b", c=K)

            with dve.Fori(0, T // UNROLL) as i:
                t = i * UNROLL
                for u in range(UNROLL):
                    q = u % 2
                    step = t + u + 1
                    dve.wait_ge(f_mm, step)
                    nc.vector.tensor_reduce(by_chunk(pre_f[:, :]), parts_of(GATE_F, q), AX.X, ALU.add).then_inc(f_sum, 1)
                    dve.wait_ge(g_mm, step)
                    nc.vector.tensor_reduce(by_chunk(pre_g[:, :]), parts_of(GATE_G, q), AX.X, ALU.add).then_inc(g_sum, 1)
                    dve.wait_ge(f_act, step)
                    nc.vector.tensor_tensor(scan_b[:, :, 1], sig_f[:, :], cell[:, :, 1], ALU.mult).then_inc(fc_done, 1)
                    dve.wait_ge(i_act, step)
                    dve.wait_ge(fc_done, step)
                    nc.vector.tensor_tensor_scan(cell[:, :, :].rearrange("p c s -> p (c s)"), scan_a[:, :, :].rearrange("p c s -> p (c s)"),
                                                 scan_b[:, :, :].rearrange("p c s -> p (c s)"), 0.0, ALU.mult, ALU.add).then_inc(c_done, 1)
                    dve.wait_ge(t_done, step)
                    nc.vector.scalar_tensor_tensor(out=hp[:, :, 0, :], in0=by_chunk(sig_o[:, :]), scalar=2.0 ** H_SCALE,
                                                   in1=by_chunk(tanh_c[:, :]), op0=ALU.mult, op1=ALU.mult).then_inc(h_hi, 1)
                    if u % HALF == 0:
                        dve.wait_ge(hring_saved, 2 * i + u // HALF + 1)
                    nc.vector.scalar_tensor_tensor(out=hring[:, u, :], in0=sig_o[:, :], scalar=2.0 ** H_SCALE,
                                                   in1=tanh_c[:, :], op0=ALU.mult, op1=ALU.mult).then_inc(h_all, 1)
                    dve.wait_ge(h_all, step)
                    nc.vector.tensor_tensor(hp[:, :, 1, :], by_chunk(hring[:, u, :]), hp[:, :, 0, :], ALU.subtract).then_inc(h_lo, 1)

            for j in range(B * NT):
                dve.wait_ge(y_filled, j + 1)
                nc.vector.tensor_copy(y_rows[:, j, 0:P], banks[2 * (j % 4)][:, 0:P]).then_inc(y_dve, 1)

        @block.scalar
        def _(act):
            act.dma_start(wh_sb[:, :, :], wh.rearrange("(k p) o -> p k o", p=P)).then_inc(s_wh, 16)
            act.dma_start(wx_sb[:, :, :], wx.rearrange("(k p) o -> p k o", p=P)).then_inc(s_wx, 16)

            def group(what):
                act.wait_ge(s_filled, order[what] + 1)
                return bank_of(what)

            bank = group(("small",))
            nc.scalar.copy(small[:, :], bank[:, 0:NSMALL]).then_inc(s_act, 1)
            for b in range(B):
                for n in range(NB):
                    bank = group(("xt", b, 1, n))
                    nc.scalar.copy(xt[:, 1, b, n * BANK:(n + 1) * BANK], bank[:, :]).then_inc(s_act, 1)
            act.wait_ge(*read_out(order[("var",)]))
            nc.scalar.activation(root[:, :], var[:, :], ACT.Sqrt).then_inc(s_var, 1)
            act.wait_ge(s_bias, 1)
            for n in range(NB):
                for b in range(B):
                    for m in range(1, M, 2):
                        bank = group(("xw", b, m, n))
                        nc.scalar.activation(xw[:, m, b, n * BANK:(n + 1) * BANK], bank[:, :], ACT.Identity,
                                             bias=bias_s[:, m:m + 1], scale=scales[:, 0:1]).then_inc(s_act, 1)

            unscale = act.alloc_register("unscale")
            act.reg_load(unscale, scales[0:1, 1:2].bitcast(U32))

            with act.Fori(0, T // UNROLL) as i:
                t = i * UNROLL
                for u in range(UNROLL):
                    q = u % 2
                    step = t + u + 1
                    act.wait_ge(f_sum, step)
                    nc.scalar.activation(sig_f[:, :], pre_f[:, :], ACT.Sigmoid, scale=unscale).then_inc(f_act, 1)
                    act.wait_ge(g_sum, step)
                    nc.scalar.activation(scan_b[:, :, 0], pre_g[:, :], ACT.Tanh, scale=unscale).then_inc(g_act, 1)
                    act.wait_ge(i_mm, step)
                    nc.scalar.activation(scan_a[:, :, 1], banks[4 * q + GATE_I][:, 0:CB], ACT.Sigmoid, scale=unscale).then_inc(i_act, 1)
                    act.wait_ge(o_mm, step)
                    nc.scalar.activation(sig_o[:, :], banks[4 * q + GATE_O][:, 0:CB], ACT.Sigmoid, scale=unscale).then_inc(o_act, 1)
                    act.wait_ge(c_done, step)
                    nc.scalar.activation(tanh_c[:, :], cell[:, :, 1], ACT.Tanh).then_inc(t_done, 1)

            for j in range(B * NT):
                act.wait_ge(y_filled, j + 1)
                nc.scalar.copy(y_rows[:, j, P:D], banks[2 * (j % 4) + 1][:, 0:P]).then_inc(y_act, 1)


_INS = ['x', 'cond_1024', 'L0_cond_weight', 'L1_cond_Wx', 'L1_cond_Wh', 'L1_cond_b']
_OUTS = [((2, 1024, 256), 'float32')]


def kernel(**inputs):
    import numpy as _np
    import concourse.bacc as _bacc
    from concourse import mybir as _mybir
    from concourse.bass_utils import run_bass_kernel_spmd as _run

    nc = _bacc.Bacc("TRN2", target_bir_lowering=False, num_devices=1)
    arrays, args = {}, []
    for name in _INS:
        a = _np.ascontiguousarray(inputs[name])
        arrays[f"in_{name}_dram"] = a
        args.append(nc.dram_tensor(f"in_{name}_dram", a.shape, _mybir.dt.from_np(a.dtype), kind="ExternalInput").ap())
    for i, (shape, dtype) in enumerate(_OUTS):
        dt = _mybir.dt.from_np(_np.dtype(dtype))
        args.append(nc.dram_tensor(f"out_{i}_dram", shape, dt, kind="ExternalOutput").ap())
    cond_resid_lstm(nc, *args)
    r = _run(nc, [arrays], core_ids=[0])
    got = tuple(r.results[0][f"out_{i}_dram"] for i in range(len(_OUTS)))
    return got[0]
```

```python
from contextlib import ExitStack

import concourse.bass as bass
from concourse import mybir

F32 = mybir.dt.float32
F16 = mybir.dt.float16
BF16 = mybir.dt.bfloat16
U32 = mybir.dt.uint32
ALU = mybir.AluOpType
ACT = mybir.ActivationFunctionType
AX = mybir.AxisListType

P = 128
BANK = 512
UNROLL = 8
HALF = UNROLL // 2
EPS = 1e-8
H_SCALE = 12
W_TOP = 14
EXPONENT = 0x7F800000
GATE_I, GATE_F, GATE_O, GATE_G = range(4)
O_REST = 7


def cond_resid_lstm(nc, x, cond, w, wx, wh, bias, out):
    B, T, D = x.shape
    K = D // P
    M = wx.shape[1] // P
    G = M // K
    CB = K * B
    NT = T // P
    NB = T // BANK
    NSMALL = B * K + M
    assert D == K * P and G == 4 and T % BANK == 0 and T % UNROLL == 0

    with ExitStack() as ctx:
        def sb(name, shape, dt=F32):
            return ctx.enter_context(nc.sbuf_tensor(name, shape, dt))

        def sem(name):
            return ctx.enter_context(nc.semaphore(name))

        x_rows = sb("x_rows", [P, B * NT, D])
        w_sb = sb("w_sb", [P, K, D])
        wx_sb = sb("wx_sb", [P, K, G * D])
        wh_sb = sb("wh_sb", [P, K, G * D])
        small_rows = sb("small_rows", [NSMALL, P])
        ident = sb("ident", [P, P])
        ident_b = sb("ident_b", [P, P], BF16)
        ones_row = sb("ones_row", [1, P])
        small = sb("small", [P, NSMALL])
        ys = sb("ys", [P, B, K])
        ys2 = sb("ys2", [P, B, K])
        w2 = sb("w2", [P, K, D])
        wy = sb("wy", [P, B, K, D])
        var = sb("var", [P, CB])
        root = sb("root", [P, CB])
        d0 = sb("d0", [P, CB])
        d_tmp = sb("d_tmp", [P, 3, CB])
        d_sb = sb("d_sb", [P, CB])
        wmax = sb("wmax", [P, 1])
        wmax1 = sb("wmax1", [1, 2])
        scales_row = sb("scales_row", [1, 2])
        scales = sb("scales", [P, 2])
        w_scale = sb("w_scale", [P, 1])
        bias_s = sb("bias_s", [P, M])
        h0wh = sb("h0wh", [P, M, B])
        xt = sb("xt", [P, K, B, T])
        xw = sb("xw", [P, M, B, T])
        wh_s = sb("wh_s", [P, K, G * D])
        wh_p = sb("wh_p", [P, 2, K, G * D], F16)

        ring = sb("ring", [P, UNROLL, G, 3, CB], BF16)
        rest = sb("rest", [P, M * B, HALF])
        hring = sb("hring", [P, UNROLL, CB])
        sig_f = sb("sig_f", [P, CB])
        scan_a = sb("scan_a", [P, CB, 2])
        scan_b = sb("scan_b", [P, CB, 2])
        scan_h = sb("scan_h", [P, CB, 3])
        h_parts = sb("h_parts", [P, 2, CB, 3], F16)
        y_rows = sb("y_rows", [P, B * NT, D])

        banks = [ctx.enter_context(nc.psum_tensor(f"bank{i}", [P, BANK], F32)) for i in range(8)]
        pre_f = banks[4][:, 0:CB]
        pre_o = banks[4][:, CB:CB + B]
        pre_g = banks[5][:, 0:CB]
        cell = banks[6][:, 0:2 * CB].rearrange("p (c s) -> p c s", s=2)

        s_x = [sem(f"s_x{b}") for b in range(B)]
        s_w, s_wx, s_wh, s_small = sem("s_w"), sem("s_wx"), sem("s_wh"), sem("s_small")
        s_zero, s_ident, s_identb, s_ones = sem("s_zero"), sem("s_ident"), sem("s_identb"), sem("s_ones")
        s_filled = sem("s_filled")
        s_act, s_dve = sem("s_act"), sem("s_dve")
        s_ys, s_ys2, s_w2, s_wy = sem("s_ys"), sem("s_ys2"), sem("s_w2"), sem("s_wy")
        s_wmax, s_scales = sem("s_wmax"), sem("s_scales")
        s_chain = sem("s_chain")
        s_bias, s_var, s_whs, s_hi = sem("s_bias"), sem("s_var"), sem("s_whs"), sem("s_hi")
        s_table = sem("s_table")
        s_setup = sem("s_setup")
        s_pool = sem("s_pool")
        ring_full, ring_used = sem("ring_full"), sem("ring_used")
        hring_saved, h_seen = sem("hring_saved"), sem("h_seen")
        h_hi, h_lo, h_all = sem("h_hi"), sem("h_lo"), sem("h_all")
        f_mm, g_mm, i_mm = sem("f_mm"), sem("g_mm"), sem("i_mm")
        o0_mm, o_mm = sem("o0_mm"), sem("o_mm")
        f_sum, g_sum, o0_sum = sem("f_sum"), sem("g_sum"), sem("o0_sum")
        f_act, i_act, o0_act, o_act = sem("f_act"), sem("i_act"), sem("o0_act"), sem("o_act")
        cell_in, c_done, t_done = sem("cell_in"), sem("c_done"), sem("t_done")
        y_filled, y_act, y_dve, s_out = sem("y_filled"), sem("y_act"), sem("y_dve"), sem("s_out")

        groups = [(("small",), "act"), (("wmax",), "dve")]
        groups += [(("xt", b, k, n), "act" if k else "dve") for b in range(B) for n in range(NB) for k in range(K)]
        groups += [(("var",), "dve"), (("scales",), "dve"), (("h0wh",), "dve")]
        groups += [(("x1", b, m, n), "dve") for b in range(B) for n in range(NB) for m in range(K)]
        groups += [(("xw", b, m, n), "act" if m % 2 else "dve") for n in range(NB) for b in range(B) for m in range(M)]
        order = {what: g for g, (what, _) in enumerate(groups)}

        def bank_of(what):
            return banks[order[what] % 8]

        def read_out(g):
            who = groups[g][1]
            return (s_act if who == "act" else s_dve), sum(1 for _, e in groups[:g + 1] if e == who)

        def last_read(kind):
            found = {}
            for g, (what, who) in enumerate(groups):
                if what[0] == kind:
                    found[who] = read_out(g)
            return list(found.values())

        block = ctx.enter_context(nc.Block())

        @block.sync
        def _(sp):
            sp.dma_start(small_rows[0:B * K, :], cond.rearrange("b (k p) -> (b k) p", p=P)).then_inc(s_small, 16)
            sp.dma_start(small_rows[B * K:NSMALL, :], bias.rearrange("(m p) -> m p", p=P)).then_inc(s_small, 16)
            sp.dma_start(w_sb[:, :, :], w.rearrange("(k p) o -> p k o", p=P)).then_inc(s_w, 16)
            for b in range(B):
                sp.dma_start(x_rows[:, b * NT:(b + 1) * NT, :],
                             x[b].rearrange("(n p) d -> p n d", p=P)).then_inc(s_x[b], 16)
            for j in range(B * NT):
                b, n = divmod(j, NT)
                sp.wait_ge(y_act, j + 1)
                sp.wait_ge(y_dve, j + 1)
                sp.dma_start(out[b, n * P:(n + 1) * P, :], y_rows[:, j, :]).then_inc(s_out, 16)
            sp.wait_ge(s_out, 16 * B * NT)

        @block.gpsimd
        def _(pool):
            nc.gpsimd.memset(ident[:, :], 0.0).then_inc(s_zero, 1)
            nc.gpsimd.memset(ones_row[:, :], 1.0).then_inc(s_ones, 1)
            pool.wait_ge(s_zero, 1)
            nc.gpsimd.affine_select(out=ident[:, :], in_=ident[:, :], compare_op=ALU.not_equal, fill=1.0,
                                    base=0, pattern=[[-1, P]], channel_multiplier=1).then_inc(s_ident, 1)
            pool.wait_ge(s_ident, 1)
            nc.gpsimd.tensor_copy(ident_b[:, :], ident[:, :]).then_inc(s_identb, 1)

            xw_t = xw[:, :, :, :].rearrange("p m b t -> p (m b) t")
            xt_t = xt[:, :, :, :].rearrange("p k b t -> p (k b) t")

            def parts(half, part):
                return ring[:, half * HALF:(half + 1) * HALF, :, part, :].rearrange("p s g c -> p g c s")

            def by_gate(ap):
                return ap.rearrange("p (g c) s -> p g c s", g=G)

            def settle():
                pool.wait_ge(s_pool, 1)
                pool.sem_inc(s_pool, -1)

            def split(half, t0):
                src = by_gate(xw_t[:, :, bass.ds(t0, HALF)])
                res = by_gate(rest[:, :, :])
                nc.gpsimd.tensor_copy(parts(half, 0), src).then_inc(s_pool, 1)
                settle()
                nc.gpsimd.tensor_tensor(res, src, parts(half, 0), ALU.subtract).then_inc(s_pool, 1)
                settle()
                nc.gpsimd.tensor_copy(parts(half, 1), res).then_inc(s_pool, 1)
                settle()
                nc.gpsimd.tensor_tensor(parts(half, 2), res, parts(half, 1), ALU.subtract).then_inc(ring_full, 1)

            def save(half, t0):
                now = xt_t[:, :, bass.ds(t0, HALF)]
                nc.gpsimd.tensor_tensor(now, now, hring[:, half * HALF:(half + 1) * HALF, :].rearrange("p s c -> p c s"),
                                        ALU.add).then_inc(hring_saved, 1)

            nc.gpsimd.memset(rest[:, 0, 0:1], 0.0).then_inc(hring_saved, 2)
            for s, v in last_read("xw"):
                pool.wait_ge(s, v)
            pool.wait_ge(s_setup, 1)
            split(0, 0)
            split(1, HALF)
            with pool.Fori(0, T // UNROLL - 1) as i:
                t = i * UNROLL
                for half in range(2):
                    pool.wait_ge(ring_used, 1)
                    pool.sem_inc(ring_used, -1)
                    split(half, t + UNROLL + half * HALF)
                    pool.wait_ge(h_all, t + (half + 1) * HALF)
                    pool.sem_inc(h_seen, 1)
                    save(half, t + half * HALF)
            for half in range(2):
                pool.wait_ge(h_all, T - UNROLL + (half + 1) * HALF)
                save(half, T - UNROLL + half * HALF)

        @block.tensor
        def _(pe):
            def start_group(what):
                g = order[what]
                if g >= 8:
                    pe.wait_ge(*read_out(g - 8))
                return banks[g % 8]

            def mm(out_, lhs, rhs, first, last):
                return nc.tensor.matmul(out_, lhs, rhs, start=first, stop=last, skip_group_check=True)

            pe.wait_ge(s_ident, 1)
            pe.wait_ge(s_small, 32)
            nc.tensor.transpose(start_group(("small",))[:, 0:NSMALL], small_rows[:, :],
                                ident[0:NSMALL, 0:NSMALL]).then_inc(s_filled, 1)
            pe.wait_ge(s_wmax, 1)
            nc.tensor.transpose(start_group(("wmax",))[0:1, 0:P], wmax[:, :], ident[:, :]).then_inc(s_filled, 1)
            for b in range(B):
                pe.wait_ge(s_x[b], 16)
                for n in range(NB):
                    for k in range(K):
                        bank = start_group(("xt", b, k, n))
                        for j in range(BANK // P):
                            last = nc.tensor.transpose(bank[:, j * P:(j + 1) * P],
                                                       x_rows[:, b * NT + n * (BANK // P) + j, k * P:(k + 1) * P], ident[:, :])
                        last.then_inc(s_filled, 1)
            bank = start_group(("var",))
            pe.wait_ge(s_ys2, 1)
            pe.wait_ge(s_w2, 1)
            for m in range(K):
                for k in range(K):
                    last = mm(bank[:, m * B:(m + 1) * B], w2[:, k, m * P:(m + 1) * P], ys2[:, :, k], m == 0 and k == 0, k == K - 1)
            last.then_inc(s_filled, 1)
            bank = start_group(("scales",))
            pe.wait_ge(s_scales, 2)
            pe.wait_ge(s_ones, 1)
            mm(bank[:, 0:2], ones_row[:, :], scales_row[:, :], True, True).then_inc(s_filled, 1)
            bank = start_group(("h0wh",))
            pe.wait_ge(s_wh, 16)
            pe.wait_ge(*read_out(order[("small",)]))
            h0 = small[:, 0:B * K].rearrange("p (b k) -> p b k", k=K)
            for m in range(M):
                for k in range(K):
                    last = mm(bank[:, m * B:(m + 1) * B], wh_sb[:, k, m * P:(m + 1) * P], h0[:, :, k], m == 0 and k == 0, k == K - 1)
            last.then_inc(s_filled, 1)
            pe.wait_ge(s_wy, B * K)
            for s, v in last_read("xt"):
                pe.wait_ge(s, v)
            for b in range(B):
                for n in range(NB):
                    for m in range(K):
                        bank = start_group(("x1", b, m, n))
                        for k in range(K):
                            last = mm(bank[:, :], wy[:, b, k, m * P:(m + 1) * P], xt[:, k, b, n * BANK:(n + 1) * BANK], k == 0, k == K - 1)
                        last.then_inc(s_filled, 1)
            pe.wait_ge(s_wx, 16)
            for n in range(NB):
                for b in range(B):
                    for m in range(M):
                        bank = start_group(("xw", b, m, n))
                        if m == 0:
                            pe.wait_ge(*read_out(order[("x1", b, K - 1, n)]))
                        for k in range(K):
                            last = mm(bank[:, :], wx_sb[:, k, m * P:(m + 1) * P], xt[:, k, b, n * BANK:(n + 1) * BANK], k == 0, k == K - 1)
                        last.then_inc(s_filled, 1)

            for s, v in last_read("xw"):
                pe.wait_ge(s, v)
            pe.wait_ge(s_setup, 1)
            pe.wait_ge(s_identb, 1)

            def apart(gate, first, last):
                return banks[gate][:, 2 * B * first:2 * B * last].rearrange("p (c q b) -> p c q b", q=2, b=B)

            def together(bank, first, last):
                return banks[bank][:, B * first:B * last].rearrange("p (c b) -> p c b", b=B)

            def in_ring(gate, u, part, first, last):
                return ring[:, u, gate, part, B * first:B * last].rearrange("p (c b) -> p c b", b=B)

            def input_apart(gate, u, first, last):
                columns = apart(gate, first, last)
                mm(columns.rearrange("p c q b -> p q c b"), ident_b[:, :],
                   ring[:, u, gate, 0:2, B * first:B * last].rearrange("p q (c b) -> p q c b", b=B), True, True)
                return mm(columns[:, :, 0, :], ident_b[:, :], in_ring(gate, u, 2, first, last), False, True)

            def input_together(gate, bank, u, first, last):
                for part in range(3):
                    mm_ = mm(together(bank, first, last), ident_b[:, :], in_ring(gate, u, part, first, last), part == 0, True)
                return mm_

            def products(gate, bank, h_part, first, last):
                for c in range(first, last):
                    m = gate * K + c
                    for k in range(K):
                        for w_part in range(2):
                            mm_ = mm(together(bank, c, c + 1)[:, 0, :], wh_p[:, w_part, k, m * P:(m + 1) * P],
                                     h_parts[:, h_part, k * B:(k + 1) * B, 2], False, True)
                return mm_

            def products_apart(gate, first, last):
                for c in range(first, last):
                    m = gate * K + c
                    for k in range(K):
                        for w_part in range(2):
                            mm_ = mm(apart(gate, c, c + 1)[:, 0, :, :], wh_p[:, w_part, k, m * P:(m + 1) * P],
                                     h_parts[:, :, k * B:(k + 1) * B, 2], False, True)
                return mm_

            for gate_mm in (f_mm, g_mm, i_mm, o0_mm, o_mm):
                pe.sem_inc(gate_mm, 1)

            with pe.Fori(0, T // UNROLL) as i:
                t = i * UNROLL
                for u in range(UNROLL):
                    if u % HALF == 0:
                        pe.wait_ge(ring_full, 2 * i + u // HALF + 1)
                    pe.wait_ge(c_done, t + u + 1)
                    input_apart(GATE_F, u, 0, K)
                    input_apart(GATE_G, u, 0, K)
                    input_together(GATE_I, GATE_I, u, 0, K)
                    pe.wait_ge(o_act, t + u + 1)
                    input_apart(GATE_O, u, 0, 1)
                    last = input_together(GATE_O, O_REST, u, 1, K)
                    if u % HALF == HALF - 1:
                        last.then_inc(ring_used, 1)
                    pe.wait_ge(h_hi, t + u + 1)
                    products(GATE_I, GATE_I, 0, 0, K)
                    pe.wait_ge(h_lo, t + u + 1)
                    products_apart(GATE_F, 0, K).then_inc(f_mm, 1)
                    products_apart(GATE_G, 0, K).then_inc(g_mm, 1)
                    products(GATE_I, GATE_I, 1, 0, K).then_inc(i_mm, 1)
                    products_apart(GATE_O, 0, 1).then_inc(o0_mm, 1)
                    products(GATE_O, O_REST, 0, 1, K)
                    products(GATE_O, O_REST, 1, 1, K).then_inc(o_mm, 1)

            pe.wait_ge(hring_saved, 2 + T // HALF)
            for j in range(B * NT):
                b, n = divmod(j, NT)
                if j >= 4:
                    pe.wait_ge(y_act, j - 3)
                    pe.wait_ge(y_dve, j - 3)
                for k in range(K):
                    last = nc.tensor.transpose(banks[2 * (j % 4) + k][:, 0:P], xt[:, k, b, n * P:(n + 1) * P], ident[:, :])
                last.then_inc(y_filled, 1)

        @block.vector
        def _(dve):
            chain = [0]

            def link(ins):
                chain[0] += 1
                ins.then_inc(s_chain, 1)
                dve.wait_ge(s_chain, chain[0])

            def group(what):
                dve.wait_ge(s_filled, order[what] + 1)
                return bank_of(what)

            dve.wait_ge(s_wh, 16)
            nc.vector.tensor_reduce(wmax[:, :], wh_sb[:, :, :], AX.XY, ALU.max, apply_absolute_value=True).then_inc(s_wmax, 1)
            dve.wait_ge(s_w, 16)
            nc.vector.tensor_tensor(w2[:, :, :], w_sb[:, :, :], w_sb[:, :, :], ALU.mult).then_inc(s_w2, 1)
            dve.wait_ge(*read_out(order[("small",)]))
            link(nc.vector.tensor_scalar(ys[:, :, :], small[:, 0:B * K].rearrange("p (b k) -> p b k", k=K),
                                         1.0 / float(D) ** 0.5, None, ALU.mult))
            nc.vector.tensor_tensor(ys2[:, :, :], ys[:, :, :], ys[:, :, :], ALU.mult).then_inc(s_ys2, 1)
            for b in range(B):
                for k in range(K):
                    nc.vector.tensor_scalar(wy[:, b, k, :], w_sb[:, k, :], ys[:, b, k:k + 1], None, ALU.mult).then_inc(s_wy, 1)
            bank = group(("wmax",))
            nc.vector.tensor_reduce(wmax1[:, 0:1], bank[0:1, 0:P], AX.X, ALU.max).then_inc(s_dve, 1)
            dve.wait_ge(*read_out(order[("wmax",)]))
            link(nc.vector.tensor_scalar(wmax1[:, 0:1], wmax1[:, 0:1], 4.0, None, ALU.max))
            link(nc.vector.tensor_scalar(wmax1[:, 0:1].bitcast(U32), wmax1[:, 0:1].bitcast(U32), EXPONENT, None, ALU.bitwise_and))
            link(nc.vector.tensor_scalar(wmax1[:, 1:2].bitcast(U32), wmax1[:, 0:1].bitcast(U32), EXPONENT, None, ALU.bitwise_xor))
            nc.vector.tensor_scalar(scales_row[:, 0:1], wmax1[:, 1:2], 2.0 ** (W_TOP - 1 + H_SCALE), None, ALU.mult).then_inc(s_scales, 1)
            nc.vector.tensor_scalar(scales_row[:, 1:2], wmax1[:, 0:1], 2.0 ** -(W_TOP + H_SCALE), None, ALU.mult).then_inc(s_scales, 1)
            for b in range(B):
                for n in range(NB):
                    bank = group(("xt", b, 0, n))
                    nc.vector.tensor_copy(xt[:, 0, b, n * BANK:(n + 1) * BANK], bank[:, :]).then_inc(s_dve, 1)
            bank = group(("var",))
            nc.vector.tensor_scalar(var[:, :], bank[:, 0:CB], EPS, None, ALU.add).then_inc(s_dve, 1)
            dve.wait_ge(*read_out(order[("var",)]))
            bank = group(("scales",))
            nc.vector.tensor_copy(scales[:, :], bank[:, 0:2]).then_inc(s_dve, 1)
            dve.wait_ge(*read_out(order[("scales",)]))
            link(nc.vector.tensor_scalar(w_scale[:, :], scales[:, 0:1], 2.0 ** -H_SCALE, None, ALU.mult))
            nc.vector.tensor_scalar(bias_s[:, :], small[:, B * K:NSMALL], scales[:, 0:1], None, ALU.mult).then_inc(s_bias, 1)
            bank = group(("h0wh",))
            nc.vector.tensor_copy(h0wh[:, :, :], bank[:, 0:M * B].rearrange("p (m b) -> p m b", b=B)).then_inc(s_dve, 1)
            dve.wait_ge(s_var, 1)
            link(nc.vector.reciprocal(d0[:, :], root[:, :]))
            link(nc.vector.tensor_tensor(d_tmp[:, 0, :], d0[:, :], d0[:, :], ALU.mult))
            link(nc.vector.tensor_tensor(d_tmp[:, 1, :], d_tmp[:, 0, :], var[:, :], ALU.mult))
            link(nc.vector.tensor_scalar(d_tmp[:, 2, :], d_tmp[:, 1, :], -0.5, 1.5, ALU.mult, ALU.add))
            link(nc.vector.tensor_tensor(d_sb[:, :], d_tmp[:, 2, :], d0[:, :], ALU.mult))
            for b in range(B):
                for n in range(NB):
                    dve.wait_ge(s_filled, order[("x1", b, K - 1, n)] + 1)
                    for s, v in last_read("xt"):
                        dve.wait_ge(s, v)
                    for m in range(K):
                        now = xt[:, m, b, n * BANK:(n + 1) * BANK]
                        nc.vector.scalar_tensor_tensor(out=now, in0=bank_of(("x1", b, m, n))[:, :], scalar=d_sb[:, m * B + b:m * B + b + 1],
                                                       in1=now, op0=ALU.mult, op1=ALU.add).then_inc(s_dve, 1)
            link(nc.vector.tensor_scalar(wh_s[:, :, :], wh_sb[:, :, :], w_scale[:, :], None, ALU.mult))
            link(nc.vector.tensor_copy(wh_p[:, 0, :, :], wh_s[:, :, :]))
            link(nc.vector.tensor_tensor(wh_p[:, 1, :, :], wh_s[:, :, :], wh_p[:, 0, :, :], ALU.subtract))
            dve.wait_ge(s_bias, 1)
            for n in range(NB):
                for b in range(B):
                    for m in range(0, M, 2):
                        bank = group(("xw", b, m, n))
                        nc.vector.tensor_scalar(xw[:, m, b, n * BANK:(n + 1) * BANK], bank[:, :], scales[:, 0:1],
                                                bias_s[:, m:m + 1], ALU.mult, ALU.add).then_inc(s_dve, 1)
            link(nc.vector.memset(scan_a[:, :, :], 0.0))
            link(nc.vector.memset(scan_h[:, :, :], 0.0))
            link(nc.vector.memset(h_parts[:, :, :, :], 0.0))
            nc.vector.memset(h_parts[:, 0, :, 0], -2.0 ** H_SCALE).then_inc(h_hi, 1)
            dve.wait_ge(h_hi, 1)
            for s, v in last_read("xw"):
                dve.wait_ge(s, v)
            nc.vector.memset(pre_f, 0.0).then_inc(h_lo, 1)
            nc.vector.memset(cell, 0.0).then_inc(c_done, 1)
            nc.vector.scalar_tensor_tensor(out=xw[:, :, :, 0], in0=h0wh[:, :, :], scalar=scales[:, 0:1],
                                           in1=xw[:, :, :, 0], op0=ALU.mult, op1=ALU.add).then_inc(s_setup, 1)

            def parts_of(gate, chunks):
                return banks[gate][:, 0:2 * B * chunks].rearrange("p (c q b) -> p c b q", b=B, q=2)

            def by_chunk(ap):
                return ap.rearrange("p (c b) -> p c b", b=B)

            def flat(ap):
                return ap.rearrange("p c s -> p (c s)")

            dve.sem_inc(f_sum, 1)
            dve.sem_inc(g_sum, 1)
            dve.sem_inc(o0_sum, 1)

            with dve.Fori(0, T // UNROLL) as i:
                t = i * UNROLL
                for u in range(UNROLL):
                    step = dve.snap(t + u + 2)
                    both = dve.snap((t + u + 1) * 2)
                    dve.wait_ge(f_mm, step)
                    nc.vector.tensor_reduce(by_chunk(pre_f), parts_of(GATE_F, K), AX.X, ALU.add).then_inc(f_sum, 1)
                    dve.wait_ge(g_mm, step)
                    nc.vector.tensor_reduce(by_chunk(pre_g), parts_of(GATE_G, K), AX.X, ALU.add).then_inc(g_sum, 1)
                    dve.wait_ge(f_act, step)
                    nc.vector.tensor_tensor(scan_b[:, :, 1], sig_f[:, :], cell[:, :, 1], ALU.mult).then_inc(cell_in, 1)
                    dve.wait_ge(o0_mm, step)
                    nc.vector.tensor_reduce(by_chunk(pre_o), parts_of(GATE_O, 1), AX.X, ALU.add).then_inc(o0_sum, 1)
                    dve.wait_ge(cell_in, both)
                    nc.vector.tensor_tensor_scan(flat(cell), flat(scan_a[:, :, :]), flat(scan_b[:, :, :]),
                                                 0.0, ALU.mult, ALU.add).then_inc(c_done, 1)
                    dve.wait_ge(t_done, step)
                    nc.vector.scalar_tensor_tensor(out=h_parts[:, 0, :, 2], in0=scan_h[:, :, 1], scalar=2.0 ** H_SCALE,
                                                   in1=scan_h[:, :, 2], op0=ALU.mult, op1=ALU.mult).then_inc(h_hi, 1)
                    dve.wait_ge(h_hi, step)
                    nc.vector.tensor_tensor_scan(flat(h_parts[:, 1, :, :]), flat(scan_h[:, :, :]), flat(h_parts[:, 0, :, :]),
                                                 0.0, ALU.mult, ALU.subtract).then_inc(h_lo, 1)
                    if u % HALF == 0:
                        dve.wait_ge(hring_saved, 2 * i + u // HALF + 1)
                    nc.vector.tensor_tensor(hring[:, u, :], scan_h[:, :, 1], scan_h[:, :, 2], ALU.mult).then_inc(h_all, 1)

            for j in range(B * NT):
                dve.wait_ge(y_filled, j + 1)
                nc.vector.tensor_copy(y_rows[:, j, 0:P], banks[2 * (j % 4)][:, 0:P]).then_inc(y_dve, 1)

        @block.scalar
        def _(act):
            act.dma_start(wh_sb[:, :, :], wh.rearrange("(k p) o -> p k o", p=P)).then_inc(s_wh, 16)
            act.dma_start(wx_sb[:, :, :], wx.rearrange("(k p) o -> p k o", p=P)).then_inc(s_wx, 16)

            def group(what):
                act.wait_ge(s_filled, order[what] + 1)
                return bank_of(what)

            bank = group(("small",))
            nc.scalar.copy(small[:, :], bank[:, 0:NSMALL]).then_inc(s_act, 1)
            for b in range(B):
                for n in range(NB):
                    bank = group(("xt", b, 1, n))
                    nc.scalar.copy(xt[:, 1, b, n * BANK:(n + 1) * BANK], bank[:, :]).then_inc(s_act, 1)
            act.wait_ge(*read_out(order[("var",)]))
            nc.scalar.activation(root[:, :], var[:, :], ACT.Sqrt).then_inc(s_var, 1)
            act.wait_ge(s_bias, 1)
            for n in range(NB):
                for b in range(B):
                    for m in range(1, M, 2):
                        bank = group(("xw", b, m, n))
                        nc.scalar.activation(xw[:, m, b, n * BANK:(n + 1) * BANK], bank[:, :], ACT.Identity,
                                             bias=bias_s[:, m:m + 1], scale=scales[:, 0:1]).then_inc(s_act, 1)

            unscale = act.alloc_register("unscale")
            act.reg_load(unscale, scales[0:1, 1:2].bitcast(U32))

            nc.scalar.activation(sig_f[:, 0:1], scales[:, 0:1], ACT.Sigmoid).then_inc(s_table, 1)
            nc.scalar.activation(sig_f[:, 1:2], scales[:, 0:1], ACT.Tanh).then_inc(o_act, 1)

            act.sem_inc(f_act, 1)
            act.sem_inc(t_done, 1)

            with act.Fori(0, T // UNROLL) as i:
                t = i * UNROLL
                for u in range(UNROLL):
                    step = t + u + 2
                    act.wait_ge(f_sum, step)
                    nc.scalar.activation(sig_f[:, :], pre_f, ACT.Sigmoid, scale=unscale).then_inc(f_act, 1)
                    act.wait_ge(i_mm, step)
                    nc.scalar.activation(scan_a[:, :, 1], banks[GATE_I][:, 0:CB], ACT.Sigmoid, scale=unscale).then_inc(i_act, 1)
                    act.wait_ge(g_sum, step)
                    nc.scalar.activation(scan_b[:, :, 0], pre_g, ACT.Tanh, scale=unscale).then_inc(cell_in, 1)
                    act.wait_ge(o0_sum, step)
                    nc.scalar.activation(scan_h[:, 0:B, 1], pre_o, ACT.Sigmoid, scale=unscale).then_inc(o0_act, 1)
                    act.wait_ge(o_mm, step)
                    nc.scalar.activation(scan_h[:, B:CB, 1], banks[O_REST][:, B:CB], ACT.Sigmoid, scale=unscale).then_inc(o_act, 1)
                    act.wait_ge(c_done, step)
                    nc.scalar.activation(scan_h[:, :, 2], cell[:, :, 1], ACT.Tanh).then_inc(t_done, 1)

            for j in range(B * NT):
                act.wait_ge(y_filled, j + 1)
                nc.scalar.copy(y_rows[:, j, P:D], banks[2 * (j % 4) + 1][:, 0:P]).then_inc(y_act, 1)


_INS = ['x', 'cond_1024', 'L0_cond_weight', 'L1_cond_Wx', 'L1_cond_Wh', 'L1_cond_b']
_OUTS = [((2, 1024, 256), 'float32')]


def kernel(**inputs):
    import numpy as _np
    import concourse.bacc as _bacc
    from concourse import mybir as _mybir
    from concourse.bass_utils import run_bass_kernel_spmd as _run

    nc = _bacc.Bacc("TRN2", target_bir_lowering=False, num_devices=1)
    arrays, args = {}, []
    for name in _INS:
        a = _np.ascontiguousarray(inputs[name])
        arrays[f"in_{name}_dram"] = a
        args.append(nc.dram_tensor(f"in_{name}_dram", a.shape, _mybir.dt.from_np(a.dtype), kind="ExternalInput").ap())
    for i, (shape, dtype) in enumerate(_OUTS):
        dt = _mybir.dt.from_np(_np.dtype(dtype))
        args.append(nc.dram_tensor(f"out_{i}_dram", shape, dt, kind="ExternalOutput").ap())
    cond_resid_lstm(nc, *args)
    r = _run(nc, [arrays], core_ids=[0])
    got = tuple(r.results[0][f"out_{i}_dram"] for i in range(len(_OUTS)))
    return got[0]
```

```python
from contextlib import ExitStack

import concourse.bass as bass
from concourse import mybir

F32 = mybir.dt.float32
F16 = mybir.dt.float16
BF16 = mybir.dt.bfloat16
U32 = mybir.dt.uint32
ALU = mybir.AluOpType
ACT = mybir.ActivationFunctionType
AX = mybir.AxisListType

P = 128
BANK = 512
UNROLL = 8
HALF = UNROLL // 2
EPS = 1e-8
H_SCALE = 12
W_TOP = 14
EXPONENT = 0x7F800000
GATE_I, GATE_F, GATE_O, GATE_G = range(4)
I_BANK, G_SUM, F_BANK, O_BANK, G_BANK, FO_SUM, CELL, O_REST = range(8)
BANK_OF_GATE = (I_BANK, F_BANK, O_BANK, G_BANK)


def cond_resid_lstm(nc, x, cond, w, wx, wh, bias, out):
    B, T, D = x.shape
    K = D // P
    M = wx.shape[1] // P
    G = M // K
    CB = K * B
    NT = T // P
    NB = T // BANK
    NSMALL = B * K + M
    assert D == K * P and G == 4 and T % BANK == 0 and T % UNROLL == 0

    with ExitStack() as ctx:
        def sb(name, shape, dt=F32):
            return ctx.enter_context(nc.sbuf_tensor(name, shape, dt))

        def sem(name):
            return ctx.enter_context(nc.semaphore(name))

        x_rows = sb("x_rows", [P, B * NT, D])
        w_sb = sb("w_sb", [P, K, D])
        wx_sb = sb("wx_sb", [P, K, G * D])
        wh_sb = sb("wh_sb", [P, K, G * D])
        small_rows = sb("small_rows", [NSMALL, P])
        ident = sb("ident", [P, P])
        ident_b = sb("ident_b", [P, P], BF16)
        ones_row = sb("ones_row", [1, P])
        small = sb("small", [P, NSMALL])
        ys = sb("ys", [P, B, K])
        ys2 = sb("ys2", [P, B, K])
        w2 = sb("w2", [P, K, D])
        wy = sb("wy", [P, B, K, D])
        var = sb("var", [P, CB])
        root = sb("root", [P, CB])
        d0 = sb("d0", [P, CB])
        d_tmp = sb("d_tmp", [P, 3, CB])
        d_sb = sb("d_sb", [P, CB])
        wmax = sb("wmax", [P, 1])
        wmax1 = sb("wmax1", [1, 2])
        scales_row = sb("scales_row", [1, 2])
        scales = sb("scales", [P, 2])
        w_scale = sb("w_scale", [P, 1])
        bias_s = sb("bias_s", [P, M])
        h0wh = sb("h0wh", [P, M, B])
        xt = sb("xt", [P, K, B, T])
        xw = sb("xw", [P, M, B, T])
        wh_s = sb("wh_s", [P, K, G * D])
        wh_p = sb("wh_p", [P, 2, K, G * D], F16)

        ring = sb("ring", [P, UNROLL, G, 3, CB], BF16)
        rest = sb("rest", [P, M * B, HALF])
        hring = sb("hring", [P, UNROLL, CB])
        sig_f = sb("sig_f", [P, CB])
        scan_in = sb("scan_in", [P, 6 * CB + 2 + 2])
        scan_a = scan_in[:, 0:3 * CB].rearrange("p (c s) -> p c s", s=3)
        scan_b = scan_in[:, 3 * CB + 2:6 * CB + 2].rearrange("p (c s) -> p c s", s=3)
        sig_ig = scan_in[:, 2:6 * CB + 2].rearrange("p (h c s) -> p h c s", h=2, s=3)[:, :, :, 0]
        scan_h = sb("scan_h", [P, CB, 3])
        h_parts = sb("h_parts", [P, 2, CB, 3], F16)
        y_rows = sb("y_rows", [P, B * NT, D])

        psum = ctx.enter_context(nc.psum_tensor("psum", [P, 8, BANK], F32))
        banks = [psum[:, i, :] for i in range(8)]
        pre_f = banks[FO_SUM][:, 0:CB]
        pre_o = banks[FO_SUM][:, CB:CB + B]
        pre_g = banks[G_SUM][:, 0:CB]
        pre_ig = psum[:, I_BANK:G_SUM + 1, 0:CB]
        cell = banks[CELL][:, 0:3 * CB].rearrange("p (c s) -> p c s", s=3)

        s_x = [[sem(f"s_x{b}_{n}") for n in range(NB)] for b in range(B)]
        s_w, s_wx, s_wh, s_small = sem("s_w"), sem("s_wx"), sem("s_wh"), sem("s_small")
        s_zero, s_ident, s_identb, s_ones = sem("s_zero"), sem("s_ident"), sem("s_identb"), sem("s_ones")
        s_filled = sem("s_filled")
        s_act, s_dve = sem("s_act"), sem("s_dve")
        s_ys2, s_w2, s_wy = sem("s_ys2"), sem("s_w2"), sem("s_wy")
        s_wh2, s_wx2 = sem("s_wh2"), sem("s_wx2")
        s_wmax, s_scales = sem("s_wmax"), sem("s_scales")
        s_chain = sem("s_chain")
        s_bias, s_var, s_whs = sem("s_bias"), sem("s_var"), sem("s_whs")
        s_wh_hi, s_wh_lo, s_start = sem("s_wh_hi"), sem("s_wh_lo"), sem("s_start")
        s_table = sem("s_table")
        s_pool = sem("s_pool")
        ring_full, ring_used = sem("ring_full"), sem("ring_used")
        hring_saved, pool_seen = sem("hring_saved"), sem("pool_seen")
        h_hi, h_lo, h_all = sem("h_hi"), sem("h_lo"), sem("h_all")
        f_mm, g_mm = sem("f_mm"), sem("g_mm")
        o0_mm, o_mm = sem("o0_mm"), sem("o_mm")
        f_sum, o0_sum = sem("f_sum"), sem("o0_sum")
        ig_in = sem("ig_in")
        f_act, o0_act, o_act = sem("f_act"), sem("o0_act"), sem("o_act")
        cell_in, c_done, t_done = sem("cell_in"), sem("c_done"), sem("t_done")
        y_filled, y_act, y_dve, s_out = sem("y_filled"), sem("y_act"), sem("y_dve"), sem("s_out")

        def per_bank(kind, n):
            return [((kind, b, k, n), "act" if kind == "xt" and k else "dve") for b in range(B) for k in range(K)]

        groups = [(("small",), "act"), (("var",), "dve"), (("h0wh",), "dve"), (("wmax",), "dve")]
        groups += per_bank("xt", 0) + [(("scales",), "dve")]
        for n in range(1, NB):
            groups += per_bank("xt", n)
        for n in range(NB):
            groups += per_bank("x1", n)
        groups += [(("xw", b, m, n), "act" if m % 2 else "dve") for n in range(NB) for b in range(B) for m in range(M)]
        order = {what: g for g, (what, _) in enumerate(groups)}

        def bank_of(what):
            return banks[order[what] % 8]

        def read_out(g):
            who = groups[g][1]
            return (s_act if who == "act" else s_dve), sum(1 for _, e in groups[:g + 1] if e == who)

        def last_read(kind, n=None):
            found = {}
            for g, (what, who) in enumerate(groups):
                if what[0] == kind and (n is None or what[3] == n):
                    found[who] = read_out(g)
            return list(found.values())

        block = ctx.enter_context(nc.Block())

        @block.sync
        def _(sp):
            sp.dma_start(small_rows[0:B * K, :], cond.rearrange("b (k p) -> (b k) p", p=P)).then_inc(s_small, 16)
            sp.dma_start(small_rows[B * K:NSMALL, :], bias.rearrange("(m p) -> m p", p=P)).then_inc(s_small, 16)
            sp.dma_start(wh_sb[:, :, :], wh.rearrange("(k p) o -> p k o", p=P)).then_inc(s_wh, 16)
            tiles = BANK // P
            for n in range(NB):
                for b in range(B):
                    sp.dma_start(x_rows[:, b * NT + n * tiles:b * NT + (n + 1) * tiles, :],
                                 x[b, n * BANK:(n + 1) * BANK].rearrange("(n p) d -> p n d", p=P)).then_inc(s_x[b][n], 16)
            sp.dma_start(wx_sb[:, :, :], wx.rearrange("(k p) o -> p k o", p=P)).then_inc(s_wx, 16)
            for j in range(B * NT):
                b, n = divmod(j, NT)
                sp.wait_ge(y_act, j + 1)
                sp.wait_ge(y_dve, j + 1)
                sp.dma_start(out[b, n * P:(n + 1) * P, :], y_rows[:, j, :]).then_inc(s_out, 16)
            sp.wait_ge(s_out, 16 * B * NT)

        @block.gpsimd
        def _(pool):
            nc.gpsimd.memset(ident[:, :], 0.0).then_inc(s_zero, 1)
            nc.gpsimd.memset(ones_row[:, :], 1.0).then_inc(s_ones, 1)
            pool.wait_ge(s_zero, 1)
            nc.gpsimd.affine_select(out=ident[:, :], in_=ident[:, :], compare_op=ALU.not_equal, fill=1.0,
                                    base=0, pattern=[[-1, P]], channel_multiplier=1).then_inc(s_ident, 1)
            pool.wait_ge(s_ident, 1)
            nc.gpsimd.tensor_copy(ident_b[:, :], ident[:, :]).then_inc(s_identb, 1)

            xw_t = xw[:, :, :, :].rearrange("p m b t -> p (m b) t")
            xt_t = xt[:, :, :, :].rearrange("p k b t -> p (k b) t")

            def parts(half, part):
                return ring[:, half * HALF:(half + 1) * HALF, :, part, :].rearrange("p s g c -> p g c s")

            def by_gate(ap):
                return ap.rearrange("p (g c) s -> p g c s", g=G)

            def settle():
                pool.wait_ge(s_pool, 1)
                pool.sem_inc(s_pool, -1)

            def split(half, t0):
                src = by_gate(xw_t[:, :, bass.ds(t0, HALF)])
                res = by_gate(rest[:, :, :])
                nc.gpsimd.tensor_copy(parts(half, 0), src).then_inc(s_pool, 1)
                settle()
                nc.gpsimd.tensor_tensor(res, src, parts(half, 0), ALU.subtract).then_inc(s_pool, 1)
                settle()
                nc.gpsimd.tensor_copy(parts(half, 1), res).then_inc(s_pool, 1)
                settle()
                nc.gpsimd.tensor_tensor(parts(half, 2), res, parts(half, 1), ALU.subtract).then_inc(ring_full, 1)

            def save(half, t0):
                now = xt_t[:, :, bass.ds(t0, HALF)]
                nc.gpsimd.tensor_tensor(now, now, hring[:, half * HALF:(half + 1) * HALF, :].rearrange("p s c -> p c s"),
                                        ALU.add).then_inc(hring_saved, 1)

            nc.gpsimd.memset(rest[:, 0, 0:1], 0.0).then_inc(hring_saved, 2)
            pool.wait_ge(s_wx, 16)
            nc.gpsimd.tensor_scalar(wx_sb[:, :, GATE_G * D:G * D], wx_sb[:, :, GATE_G * D:G * D], 2.0, None, ALU.mult).then_inc(s_wx2, 1)
            pool.wait_ge(s_whs, 1)
            pool.wait_ge(s_wh_hi, 1)
            nc.gpsimd.tensor_tensor(wh_p[:, 1, :, :], wh_s[:, :, :], wh_p[:, 0, :, :], ALU.subtract).then_inc(s_wh_lo, 1)
            for s, v in last_read("xw", 0):
                pool.wait_ge(s, v)
            pool.wait_ge(s_start, 1)
            split(0, 0)
            split(1, HALF)
            for s, v in last_read("xw"):
                pool.wait_ge(s, v)

            with pool.Fori(0, T // UNROLL - 1) as i:
                t = i * UNROLL
                for half in range(2):
                    pool.wait_ge(ring_used, 1)
                    pool.sem_inc(ring_used, -1)
                    split(half, t + UNROLL + half * HALF)
                    pool.wait_ge(h_all, t + (half + 1) * HALF)
                    pool.sem_inc(pool_seen, 1)
                    save(half, t + half * HALF)
            for half in range(2):
                pool.wait_ge(h_all, T - UNROLL + (half + 1) * HALF)
                save(half, T - UNROLL + half * HALF)

        @block.tensor
        def _(pe):
            def start_group(what):
                g = order[what]
                if g >= 8:
                    pe.wait_ge(*read_out(g - 8))
                return banks[g % 8]

            def mm(out_, lhs, rhs, first, last):
                return nc.tensor.matmul(out_, lhs, rhs, start=first, stop=last, skip_group_check=True)

            pe.wait_ge(s_ident, 1)
            pe.wait_ge(s_small, 32)
            nc.tensor.transpose(start_group(("small",))[:, 0:NSMALL], small_rows[:, :],
                                ident[0:NSMALL, 0:NSMALL]).then_inc(s_filled, 1)
            bank = start_group(("var",))
            pe.wait_ge(s_ys2, 1)
            pe.wait_ge(s_w2, 1)
            for m in range(K):
                for k in range(K):
                    last = mm(bank[:, m * B:(m + 1) * B], w2[:, k, m * P:(m + 1) * P], ys2[:, :, k], m == 0 and k == 0, k == K - 1)
            last.then_inc(s_filled, 1)

            def transpose_x(n):
                for b in range(B):
                    pe.wait_ge(s_x[b][n], 16)
                    for k in range(K):
                        bank = start_group(("xt", b, k, n))
                        for j in range(BANK // P):
                            last = nc.tensor.transpose(bank[:, j * P:(j + 1) * P],
                                                       x_rows[:, b * NT + n * (BANK // P) + j, k * P:(k + 1) * P], ident[:, :])
                        last.then_inc(s_filled, 1)

            def project_x(n):
                for s, v in last_read("xt", n):
                    pe.wait_ge(s, v)
                for b in range(B):
                    for m in range(K):
                        bank = start_group(("x1", b, m, n))
                        for k in range(K):
                            last = mm(bank[:, :], wy[:, b, k, m * P:(m + 1) * P], xt[:, k, b, n * BANK:(n + 1) * BANK], k == 0, k == K - 1)
                        last.then_inc(s_filled, 1)

            bank = start_group(("h0wh",))
            pe.wait_ge(s_wh2, 1)
            pe.wait_ge(*read_out(order[("small",)]))
            h0 = small[:, 0:B * K].rearrange("p (b k) -> p b k", k=K)
            for m in range(M):
                for k in range(K):
                    last = mm(bank[:, m * B:(m + 1) * B], wh_sb[:, k, m * P:(m + 1) * P], h0[:, :, k], m == 0 and k == 0, k == K - 1)
            last.then_inc(s_filled, 1)
            bank = start_group(("wmax",))
            pe.wait_ge(s_wmax, 1)
            nc.tensor.transpose(bank[0:1, 0:P], wmax[:, :], ident[:, :]).then_inc(s_filled, 1)
            transpose_x(0)
            bank = start_group(("scales",))
            pe.wait_ge(s_scales, 2)
            pe.wait_ge(s_ones, 1)
            mm(bank[:, 0:2], ones_row[:, :], scales_row[:, :], True, True).then_inc(s_filled, 1)
            for n in range(1, NB):
                transpose_x(n)
            pe.wait_ge(s_wy, B * K)
            for n in range(NB):
                project_x(n)
            pe.wait_ge(s_wx, 16)
            pe.wait_ge(s_wx2, 1)
            for n in range(NB):
                for s, v in last_read("x1", n):
                    pe.wait_ge(s, v)
                for b in range(B):
                    for m in range(M):
                        bank = start_group(("xw", b, m, n))
                        for k in range(K):
                            last = mm(bank[:, :], wx_sb[:, k, m * P:(m + 1) * P], xt[:, k, b, n * BANK:(n + 1) * BANK], k == 0, k == K - 1)
                        last.then_inc(s_filled, 1)

            for s, v in last_read("xw"):
                pe.wait_ge(s, v)
            pe.wait_ge(s_wh_hi, 1)
            pe.wait_ge(s_wh_lo, 1)
            pe.wait_ge(s_identb, 1)

            def apart(gate, first, last):
                return banks[BANK_OF_GATE[gate]][:, 2 * B * first:2 * B * last].rearrange("p (c q b) -> p c q b", q=2, b=B)

            def together(bank, first, last):
                return banks[bank][:, B * first:B * last].rearrange("p (c b) -> p c b", b=B)

            def in_ring(gate, u, part, first, last):
                return ring[:, u, gate, part, B * first:B * last].rearrange("p (c b) -> p c b", b=B)

            def input_apart(gate, u, first, last):
                columns = apart(gate, first, last)
                mm(columns.rearrange("p c q b -> p q c b"), ident_b[:, :],
                   ring[:, u, gate, 0:2, B * first:B * last].rearrange("p q (c b) -> p q c b", b=B), True, True)
                return mm(columns[:, :, 0, :], ident_b[:, :], in_ring(gate, u, 2, first, last), False, True)

            def input_together(gate, bank, u, first, last):
                for part in range(3):
                    mm_ = mm(together(bank, first, last), ident_b[:, :], in_ring(gate, u, part, first, last), part == 0, True)
                return mm_

            def products(gate, bank, h_part, first, last):
                for c in range(first, last):
                    m = gate * K + c
                    for k in range(K):
                        for w_part in range(2):
                            mm_ = mm(together(bank, c, c + 1)[:, 0, :], wh_p[:, w_part, k, m * P:(m + 1) * P],
                                     h_parts[:, h_part, k * B:(k + 1) * B, 2], False, True)
                return mm_

            def products_apart(gate, first, last):
                for c in range(first, last):
                    m = gate * K + c
                    for k in range(K):
                        for w_part in range(2):
                            mm_ = mm(apart(gate, c, c + 1)[:, 0, :, :], wh_p[:, w_part, k, m * P:(m + 1) * P],
                                     h_parts[:, :, k * B:(k + 1) * B, 2], False, True)
                return mm_

            for gate_mm in (f_mm, g_mm, o0_mm, o_mm):
                pe.sem_inc(gate_mm, 1)

            with pe.Fori(0, T // UNROLL) as i:
                t = i * UNROLL
                for u in range(UNROLL):
                    if u % HALF == 0:
                        pe.wait_ge(ring_full, 2 * i + u // HALF + 1)
                    pe.wait_ge(c_done, t + u + 1)
                    input_apart(GATE_F, u, 0, K)
                    input_apart(GATE_G, u, 0, K)
                    input_together(GATE_I, I_BANK, u, 0, K)
                    pe.wait_ge(o_act, t + u + 1)
                    input_apart(GATE_O, u, 0, 1)
                    last = input_together(GATE_O, O_REST, u, 1, K)
                    if u % HALF == HALF - 1:
                        last.then_inc(ring_used, 1)
                    pe.wait_ge(h_hi, t + u + 1)
                    products(GATE_I, I_BANK, 0, 0, K)
                    pe.wait_ge(h_lo, t + u + 1)
                    products_apart(GATE_F, 0, K).then_inc(f_mm, 1)
                    products_apart(GATE_G, 0, K).then_inc(g_mm, 1)
                    products(GATE_I, I_BANK, 1, 0, K).then_inc(ig_in, 1)
                    products_apart(GATE_O, 0, 1).then_inc(o0_mm, 1)
                    products(GATE_O, O_REST, 0, 1, K)
                    products(GATE_O, O_REST, 1, 1, K).then_inc(o_mm, 1)

            pe.wait_ge(hring_saved, 2 + T // HALF)
            for j in range(B * NT):
                b, n = divmod(j, NT)
                if j >= 4:
                    pe.wait_ge(y_act, j - 3)
                    pe.wait_ge(y_dve, j - 3)
                for k in range(K):
                    last = nc.tensor.transpose(banks[2 * (j % 4) + k][:, 0:P], xt[:, k, b, n * P:(n + 1) * P], ident[:, :])
                last.then_inc(y_filled, 1)

        @block.vector
        def _(dve):
            chain = [0]

            def link(ins):
                chain[0] += 1
                ins.then_inc(s_chain, 1)
                dve.wait_ge(s_chain, chain[0])

            def group(what):
                dve.wait_ge(s_filled, order[what] + 1)
                return bank_of(what)

            dve.wait_ge(*read_out(order[("small",)]))
            link(nc.vector.tensor_scalar(ys[:, :, :], small[:, 0:B * K].rearrange("p (b k) -> p b k", k=K),
                                         1.0 / float(D) ** 0.5, None, ALU.mult))
            nc.vector.tensor_tensor(ys2[:, :, :], ys[:, :, :], ys[:, :, :], ALU.mult).then_inc(s_ys2, 1)
            dve.wait_ge(s_w, 16)
            nc.vector.tensor_tensor(w2[:, :, :], w_sb[:, :, :], w_sb[:, :, :], ALU.mult).then_inc(s_w2, 1)
            dve.wait_ge(s_wh, 16)
            nc.vector.tensor_scalar(wh_sb[:, :, GATE_G * D:G * D], wh_sb[:, :, GATE_G * D:G * D], 2.0, None, ALU.mult).then_inc(s_wh2, 1)
            nc.vector.tensor_scalar(small[:, B * K + GATE_G * K:NSMALL], small[:, B * K + GATE_G * K:NSMALL],
                                    2.0, None, ALU.mult).then_inc(s_wh2, 1)
            dve.wait_ge(s_wh2, 2)
            nc.vector.tensor_reduce(wmax[:, :], wh_sb[:, :, :], AX.XY, ALU.max, apply_absolute_value=True).then_inc(s_wmax, 1)
            for b in range(B):
                for k in range(K):
                    nc.vector.tensor_scalar(wy[:, b, k, :], w_sb[:, k, :], ys[:, b, k:k + 1], None, ALU.mult).then_inc(s_wy, 1)
            bank = group(("var",))
            nc.vector.tensor_scalar(var[:, :], bank[:, 0:CB], EPS, None, ALU.add).then_inc(s_dve, 1)

            def read_x(n):
                for b in range(B):
                    bank = group(("xt", b, 0, n))
                    nc.vector.tensor_copy(xt[:, 0, b, n * BANK:(n + 1) * BANK], bank[:, :]).then_inc(s_dve, 1)

            def add_projection(n):
                for s, v in last_read("xt", n):
                    dve.wait_ge(s, v)
                for b in range(B):
                    dve.wait_ge(s_filled, order[("x1", b, K - 1, n)] + 1)
                    for m in range(K):
                        now = xt[:, m, b, n * BANK:(n + 1) * BANK]
                        nc.vector.scalar_tensor_tensor(out=now, in0=bank_of(("x1", b, m, n))[:, :], scalar=d_sb[:, m * B + b:m * B + b + 1],
                                                       in1=now, op0=ALU.mult, op1=ALU.add).then_inc(s_dve, 1)

            bank = group(("h0wh",))
            nc.vector.tensor_copy(h0wh[:, :, :], bank[:, 0:M * B].rearrange("p (m b) -> p m b", b=B)).then_inc(s_dve, 1)
            dve.wait_ge(s_var, 1)
            link(nc.vector.reciprocal(d0[:, :], root[:, :]))
            link(nc.vector.tensor_tensor(d_tmp[:, 0, :], d0[:, :], d0[:, :], ALU.mult))
            link(nc.vector.tensor_tensor(d_tmp[:, 1, :], d_tmp[:, 0, :], var[:, :], ALU.mult))
            link(nc.vector.tensor_scalar(d_tmp[:, 2, :], d_tmp[:, 1, :], -0.5, 1.5, ALU.mult, ALU.add))
            link(nc.vector.tensor_tensor(d_sb[:, :], d_tmp[:, 2, :], d0[:, :], ALU.mult))
            bank = group(("wmax",))
            nc.vector.tensor_reduce(wmax1[:, 0:1], bank[0:1, 0:P], AX.X, ALU.max).then_inc(s_dve, 1)
            dve.wait_ge(*read_out(order[("wmax",)]))
            link(nc.vector.tensor_scalar(wmax1[:, 0:1], wmax1[:, 0:1], 4.0, None, ALU.max))
            link(nc.vector.tensor_scalar(wmax1[:, 0:1].bitcast(U32), wmax1[:, 0:1].bitcast(U32), EXPONENT, None, ALU.bitwise_and))
            link(nc.vector.tensor_scalar(wmax1[:, 1:2].bitcast(U32), wmax1[:, 0:1].bitcast(U32), EXPONENT, None, ALU.bitwise_xor))
            nc.vector.tensor_scalar(scales_row[:, 0:1], wmax1[:, 1:2], 2.0 ** (W_TOP - 1 + H_SCALE), None, ALU.mult).then_inc(s_scales, 1)
            nc.vector.tensor_scalar(scales_row[:, 1:2], wmax1[:, 0:1], 2.0 ** -(W_TOP + H_SCALE), None, ALU.mult).then_inc(s_scales, 1)
            read_x(0)
            bank = group(("scales",))
            nc.vector.tensor_copy(scales[:, :], bank[:, 0:2]).then_inc(s_dve, 1)
            dve.wait_ge(*read_out(order[("scales",)]))
            nc.vector.tensor_scalar(w_scale[:, :], scales[:, 0:1], 2.0 ** -H_SCALE, None, ALU.mult).then_inc(s_bias, 1)
            nc.vector.tensor_scalar(bias_s[:, :], small[:, B * K:NSMALL], scales[:, 0:1], None, ALU.mult).then_inc(s_bias, 1)
            for n in range(1, NB):
                read_x(n)
            for n in range(NB):
                add_projection(n)
            link(nc.vector.memset(scan_in[:, :], 0.0))
            nc.vector.memset(scan_a[:, :, 1], 2.0)
            nc.vector.memset(scan_b[:, :, 1], -1.0)
            link(nc.vector.memset(scan_h[:, :, :], 0.0))
            link(nc.vector.memset(h_parts[:, :, :, :], 0.0))
            nc.vector.memset(h_parts[:, 0, :, 0], -2.0 ** H_SCALE).then_inc(h_hi, 1)
            dve.wait_ge(h_hi, 1)
            dve.wait_ge(s_bias, 2)
            for n in range(NB):
                for b in range(B):
                    for m in range(0, M, 2):
                        bank = group(("xw", b, m, n))
                        nc.vector.tensor_scalar(xw[:, m, b, n * BANK:(n + 1) * BANK], bank[:, :], scales[:, 0:1],
                                                bias_s[:, m:m + 1], ALU.mult, ALU.add).then_inc(s_dve, 1)
                if n == 0:
                    for s, v in last_read("xw", 0):
                        dve.wait_ge(s, v)
                    nc.vector.scalar_tensor_tensor(out=xw[:, :, :, 0], in0=h0wh[:, :, :], scalar=scales[:, 0:1],
                                                   in1=xw[:, :, :, 0], op0=ALU.mult, op1=ALU.add).then_inc(s_start, 1)
            for s, v in last_read("xw"):
                dve.wait_ge(s, v)
            nc.vector.memset(pre_f, 0.0).then_inc(h_lo, 1)
            nc.vector.memset(cell, 0.0).then_inc(c_done, 1)

            def parts_of(gate, chunks):
                return banks[BANK_OF_GATE[gate]][:, 0:2 * B * chunks].rearrange("p (c q b) -> p c b q", b=B, q=2)

            def by_chunk(ap):
                return ap.rearrange("p (c b) -> p c b", b=B)

            def flat(ap):
                return ap.rearrange("p c s -> p (c s)")

            dve.sem_inc(f_sum, 1)
            dve.sem_inc(o0_sum, 1)

            with dve.Fori(0, T // UNROLL) as i:
                t = i * UNROLL
                for u in range(UNROLL):
                    step = dve.snap(t + u + 2)
                    both = dve.snap((t + u + 1) * 2)
                    dve.wait_ge(f_mm, step)
                    nc.vector.tensor_reduce(by_chunk(pre_f), parts_of(GATE_F, K), AX.X, ALU.add).then_inc(f_sum, 1)
                    dve.wait_ge(g_mm, step)
                    nc.vector.tensor_reduce(by_chunk(pre_g), parts_of(GATE_G, K), AX.X, ALU.add).then_inc(ig_in, 1)
                    dve.wait_ge(f_act, step)
                    nc.vector.tensor_tensor(scan_b[:, :, 2], sig_f[:, :], cell[:, :, 2], ALU.mult).then_inc(cell_in, 1)
                    dve.wait_ge(o0_mm, step)
                    nc.vector.tensor_reduce(by_chunk(pre_o), parts_of(GATE_O, 1), AX.X, ALU.add).then_inc(o0_sum, 1)
                    dve.wait_ge(cell_in, both)
                    nc.vector.tensor_tensor_scan(flat(cell), flat(scan_a), flat(scan_b),
                                                 0.0, ALU.mult, ALU.add).then_inc(c_done, 1)
                    dve.wait_ge(t_done, step)
                    nc.vector.scalar_tensor_tensor(out=h_parts[:, 0, :, 2], in0=scan_h[:, :, 1], scalar=2.0 ** H_SCALE,
                                                   in1=scan_h[:, :, 2], op0=ALU.mult, op1=ALU.mult).then_inc(h_hi, 1)
                    dve.wait_ge(h_hi, step)
                    nc.vector.tensor_tensor_scan(flat(h_parts[:, 1, :, :]), flat(scan_h[:, :, :]), flat(h_parts[:, 0, :, :]),
                                                 0.0, ALU.mult, ALU.subtract).then_inc(h_lo, 1)
                    if u % HALF == 0:
                        dve.wait_ge(hring_saved, 2 * i + u // HALF + 1)
                    nc.vector.tensor_tensor(hring[:, u, :], scan_h[:, :, 1], scan_h[:, :, 2], ALU.mult).then_inc(h_all, 1)

            for j in range(B * NT):
                dve.wait_ge(y_filled, j + 1)
                nc.vector.tensor_copy(y_rows[:, j, 0:P], banks[2 * (j % 4)][:, 0:P]).then_inc(y_dve, 1)

        @block.scalar
        def _(act):
            act.dma_start(w_sb[:, :, :], w.rearrange("(k p) o -> p k o", p=P)).then_inc(s_w, 16)

            def group(what):
                act.wait_ge(s_filled, order[what] + 1)
                return bank_of(what)

            bank = group(("small",))
            nc.scalar.copy(small[:, :], bank[:, 0:NSMALL]).then_inc(s_act, 1)
            def read_x(n):
                for b in range(B):
                    bank = group(("xt", b, 1, n))
                    nc.scalar.copy(xt[:, 1, b, n * BANK:(n + 1) * BANK], bank[:, :]).then_inc(s_act, 1)

            def load_tables():
                nc.scalar.activation(sig_f[:, 0:1], scales[:, 0:1], ACT.Sigmoid).then_inc(s_table, 1)
                nc.scalar.activation(sig_f[:, 1:2], scales[:, 0:1], ACT.Tanh).then_inc(o_act, 1)

            act.wait_ge(*read_out(order[("var",)]))
            nc.scalar.activation(root[:, :], var[:, :], ACT.Sqrt).then_inc(s_var, 1)
            for n in range(NB):
                read_x(n)
            act.wait_ge(s_wh2, 1)
            act.wait_ge(s_bias, 2)
            nc.scalar.activation(wh_p[:, 0, :, :], wh_sb[:, :, :], ACT.Copy, scale=w_scale[:, :]).then_inc(s_wh_hi, 1)
            nc.scalar.activation(wh_s[:, :, :], wh_sb[:, :, :], ACT.Copy, scale=w_scale[:, :]).then_inc(s_whs, 1)
            for n in range(NB):
                for b in range(B):
                    for m in range(1, M, 2):
                        bank = group(("xw", b, m, n))
                        nc.scalar.activation(xw[:, m, b, n * BANK:(n + 1) * BANK], bank[:, :], ACT.Identity,
                                             bias=bias_s[:, m:m + 1], scale=scales[:, 0:1]).then_inc(s_act, 1)
                        if n == NB - 1 and b == B - 1 and m == 1:
                            load_tables()

            unscale = act.alloc_register("unscale")
            act.reg_load(unscale, scales[0:1, 1:2].bitcast(U32))

            act.sem_inc(f_act, 1)
            act.sem_inc(t_done, 1)

            with act.Fori(0, T // UNROLL) as i:
                t = i * UNROLL
                for u in range(UNROLL):
                    step = act.snap(t + u + 2)
                    both = act.snap((t + u + 1) * 2)
                    act.wait_ge(f_sum, step)
                    nc.scalar.activation(sig_f[:, :], pre_f, ACT.Sigmoid, scale=unscale).then_inc(f_act, 1)
                    act.wait_ge(ig_in, both)
                    nc.scalar.activation(sig_ig, pre_ig, ACT.Sigmoid, scale=unscale).then_inc(cell_in, 1)
                    act.wait_ge(o0_sum, step)
                    nc.scalar.activation(scan_h[:, 0:B, 1], pre_o, ACT.Sigmoid, scale=unscale).then_inc(o0_act, 1)
                    act.wait_ge(o_mm, step)
                    nc.scalar.activation(scan_h[:, B:CB, 1], banks[O_REST][:, B:CB], ACT.Sigmoid, scale=unscale).then_inc(o_act, 1)
                    act.wait_ge(c_done, step)
                    nc.scalar.activation(scan_h[:, :, 2], cell[:, :, 2], ACT.Tanh).then_inc(t_done, 1)

            for j in range(B * NT):
                act.wait_ge(y_filled, j + 1)
                nc.scalar.copy(y_rows[:, j, P:D], banks[2 * (j % 4) + 1][:, 0:P]).then_inc(y_act, 1)


_INS = ['x', 'cond_1024', 'L0_cond_weight', 'L1_cond_Wx', 'L1_cond_Wh', 'L1_cond_b']
_OUTS = [((2, 1024, 256), 'float32')]


def kernel(**inputs):
    import numpy as _np
    import concourse.bacc as _bacc
    from concourse import mybir as _mybir
    from concourse.bass_utils import run_bass_kernel_spmd as _run

    nc = _bacc.Bacc("TRN2", target_bir_lowering=False, num_devices=1)
    arrays, args = {}, []
    for name in _INS:
        a = _np.ascontiguousarray(inputs[name])
        arrays[f"in_{name}_dram"] = a
        args.append(nc.dram_tensor(f"in_{name}_dram", a.shape, _mybir.dt.from_np(a.dtype), kind="ExternalInput").ap())
    for i, (shape, dtype) in enumerate(_OUTS):
        dt = _mybir.dt.from_np(_np.dtype(dtype))
        args.append(nc.dram_tensor(f"out_{i}_dram", shape, dt, kind="ExternalOutput").ap())
    cond_resid_lstm(nc, *args)
    r = _run(nc, [arrays], core_ids=[0])
    got = tuple(r.results[0][f"out_{i}_dram"] for i in range(len(_OUTS)))
    return got[0]
```
